# Optimizing a Trainium2 kernel written in Bass

```python
import numpy as np
import jax
import jax.numpy as jnp

def _softmax(x, axis=-1):
    return jax.nn.softmax(x, axis=axis)

def _gelu(x):
    return jax.nn.gelu(x, approximate=True)

def _silu(x):
    return jax.nn.silu(x)

def _sigmoid(x):
    return jax.nn.sigmoid(x)

def _layernorm(x, axis=-1, eps=1e-05):
    m = jnp.mean(x, axis=axis, keepdims=True)
    v = jnp.var(x, axis=axis, keepdims=True)
    return (x - m) / jnp.sqrt(v + eps)

def _scatter_add(tgt, idx, src, axis=0):
    return tgt.at[idx].add(src)

def _segment_sum(src, seg, n):
    return jax.ops.segment_sum(src, seg, n)
kernel_name = 'mk_gnn_resnorm_d4_gnn_r32_3a6d0f'

def setup_inputs(seed: int=0):
    np.random.seed(seed)
    _w = jnp.asarray

    def _rec_inputs():
        import jax
        import jax.numpy as jnp
        _gk = jax.random.key(seed)
        x = -9.077e-06 + 0.04419 * jax.random.normal(jax.random.fold_in(_gk, 1), (10000, 512), jnp.float32)
        src = jax.random.randint(jax.random.fold_in(_gk, 2), (5000,), 0, 10000, jnp.int32)
        dst = jnp.minimum((10000 * jax.random.uniform(jax.random.fold_in(_gk, 3), (5000,)) ** 2.0).astype(jnp.int32), 9999)
        _o = jnp.argsort(dst, stable=True)
        src = src[_o]
        dst = dst[_o]
        edge_type_2 = jax.random.randint(jax.random.fold_in(_gk, 12), (5000,), 0, 2, jnp.int32)
        edge_weight = jax.random.uniform(jax.random.fold_in(_gk, 13), (5000,), jnp.float32, 0.0, 0.999998)
        return (x, src, dst, edge_type_2, edge_weight)
    x, src, dst, edge_type_2, edge_weight = _rec_inputs()

    def _L0_gnn_setup():
        import jax, jax.numpy as jnp
        import numpy as np
        EPS = 1e-12

        def _gcn_conv(x, W, b, src, dst, w, n_nodes):
            h = x @ W
            deg = jax.ops.segment_sum(w, dst, num_segments=n_nodes)
            dinv = jnp.where(deg > 0, jax.lax.rsqrt(deg), 0.0)
            norm = dinv[src] * w * dinv[dst]
            out = jax.ops.segment_sum(h[src] * norm[:, None], dst, num_segments=n_nodes)
            return out + b
        key = jax.random.key(seed)
        ks = jax.random.split(key, 6)
        N, E, F_in, F_hid, F_out = (50000, 12500, 512, 256, 512)
        node_features = jax.random.normal(ks[0], (N, F_in), dtype=jnp.float32)
        node_features = node_features / jnp.linalg.norm(node_features, axis=-1, keepdims=True)
        edge_index = jax.random.randint(ks[1], (2, E), 0, N, dtype=jnp.int64)
        edge_weight = jax.random.uniform(ks[2], (E,), dtype=jnp.float32)
        W1 = jax.random.normal(ks[3], (F_in, F_hid), dtype=jnp.float32) / np.sqrt(F_in)
        b1 = jnp.zeros((F_hid,), dtype=jnp.float32)
        W2 = jax.random.normal(ks[4], (F_hid, F_out), dtype=jnp.float32) / np.sqrt(F_hid)
        b2 = jnp.zeros((F_out,), dtype=jnp.float32)
        return {'node_features': node_features, 'edge_index': edge_index, 'edge_weight': edge_weight, 'W1': W1, 'b1': b1, 'W2': W2, 'b2': b2}
    _L0_gnn_all = _L0_gnn_setup()
    _L0_gnn_in = {k: v for k, v in _L0_gnn_all.items() if k in ('W1', 'b1', 'W2', 'b2')}
    del _L0_gnn_all

    def _L1_gnn_setup():
        import jax, jax.numpy as jnp
        import numpy as np
        NUM_RELATIONS = 2
        NUM_BASES = 30
        HIDDEN = 512
        N_NODES = 10000
        N_EDGES = 5000

        def rgcn_gate_layer(x, row, col, edge_type, basis, att, gate_w, root, bias):
            H = x.shape[1]
            w = jnp.einsum('rb,bio->rio', att, basis)
            x_j = x[col]
            msgs = []
            for r in range(NUM_RELATIONS):
                gate = jax.nn.sigmoid(x_j @ gate_w[r, :, 0])
                msgs.append(gate[:, None] * x_j @ w[r])
            msg = jnp.where((edge_type == 0)[:, None], msgs[0], msgs[1])
            agg = jax.ops.segment_sum(msg, row, num_segments=x.shape[0])
            return agg + x @ root + bias
        key = jax.random.key(seed)
        ks = jax.random.split(key, 16)
        H, R, B = (HIDDEN, NUM_RELATIONS, NUM_BASES)
        bound = 1.0 / np.sqrt(B * H)
        u = lambda k, shape: jax.random.uniform(k, shape, jnp.float32, -bound, bound)
        inp = {'x': jax.random.normal(ks[0], (N_NODES, H), jnp.float32), 'edge_index': jax.random.randint(ks[1], (2, N_EDGES), 0, N_NODES, jnp.int32), 'edge_type': jax.random.randint(ks[2], (N_EDGES,), 0, R, jnp.int32), 'basis1': u(ks[3], (B, H, H)), 'att1': u(ks[4], (R, B)), 'gate_w1': u(ks[5], (R, H, 1)), 'root1': u(ks[6], (H, H)), 'bias1': u(ks[7], (H,)), 'basis2': u(ks[8], (B, H, H)), 'att2': u(ks[9], (R, B)), 'gate_w2': u(ks[10], (R, H, 1)), 'root2': u(ks[11], (H, H)), 'bias2': u(ks[12], (H,))}
        return inp
    _L1_gnn_all = _L1_gnn_setup()
    _L1_gnn_in = {k: v for k, v in _L1_gnn_all.items() if k in ('basis1', 'att1', 'gate_w1', 'root1', 'bias1', 'basis2', 'att2', 'gate_w2', 'root2', 'bias2')}
    del _L1_gnn_all

    def _L2_gnn_setup():
        import jax, jax.numpy as jnp
        import numpy as np
        from math import sqrt
        N = 50000
        E = 25000
        D_EMB = 512
        DK = 64
        DV = 64
        HEADS = 8

        def _attention_message(Q, K, V, senders, receivers, n_nodes):
            scale = 1.0 / sqrt(Q.shape[-1])
            scores = jnp.einsum('ehd,ehd->eh', Q[receivers], K[senders]) * scale
            smax = jax.ops.segment_max(scores, receivers, num_segments=n_nodes)
            ex = jnp.exp(scores - smax[receivers])
            denom = jax.ops.segment_sum(ex, receivers, num_segments=n_nodes)
            att = ex / denom[receivers]
            out = jax.ops.segment_sum(att[:, :, None] * V[senders], receivers, num_segments=n_nodes)
            return (out, att)
        key = jax.random.key(seed)
        k1, k2, k3, k4 = jax.random.split(key, 4)
        x = jax.random.normal(k1, (N, D_EMB), dtype=jnp.float32)
        edge_index = jax.random.randint(k2, (2, E), 0, N, dtype=jnp.int64)
        out_qkv = (2 * DK + DV) * HEADS
        W_qkv = jax.random.normal(k3, (out_qkv, D_EMB), dtype=jnp.float32) / sqrt(D_EMB)
        b_qkv = jnp.zeros((out_qkv,), dtype=jnp.float32)
        W_ff = jax.random.normal(k4, (D_EMB, DV * HEADS), dtype=jnp.float32) / sqrt(DV * HEADS)
        b_ff = jnp.zeros((D_EMB,), dtype=jnp.float32)
        return {'x': x, 'edge_index': edge_index, 'W_qkv': W_qkv, 'b_qkv': b_qkv, 'W_ff': W_ff, 'b_ff': b_ff}
    _L2_gnn_all = _L2_gnn_setup()
    _L2_gnn_in = {k: v for k, v in _L2_gnn_all.items() if k in ('W_qkv', 'b_qkv', 'W_ff', 'b_ff')}
    del _L2_gnn_all

    def _L3_gnn_setup():
        import jax, jax.numpy as jnp
        import numpy as np
        N_NODES = 10000
        N_EDGES = 5000
        D_IN = 512
        D_OUT = 512
        key = jax.random.key(seed)
        k_x, k_e, k_wl, k_wr = jax.random.split(key, 4)
        x = jax.random.normal(k_x, (N_NODES, D_IN), dtype=jnp.float32)
        edge_index = jax.random.randint(k_e, (2, N_EDGES), 0, N_NODES, dtype=jnp.int64)
        scale = 1.0 / np.sqrt(D_IN)
        W_l = jax.random.normal(k_wl, (D_IN, D_OUT), dtype=jnp.float32) * scale
        W_r = jax.random.normal(k_wr, (D_IN, D_OUT), dtype=jnp.float32) * scale
        b = jnp.zeros((D_OUT,), dtype=jnp.float32)
        return {'x': x, 'edge_index': edge_index, 'W_l': W_l, 'W_r': W_r, 'b': b}
    _L3_gnn_all = _L3_gnn_setup()
    _L3_gnn_in = {k: v for k, v in _L3_gnn_all.items() if k in ('W_l', 'W_r', 'b')}
    del _L3_gnn_all
    return {'x': x, 'src': src, 'dst': dst, 'edge_type_2': edge_type_2, 'edge_weight': edge_weight, 'L0_gnn_W1': _L0_gnn_in['W1'], 'L0_gnn_b1': _L0_gnn_in['b1'], 'L0_gnn_W2': _L0_gnn_in['W2'], 'L0_gnn_b2': _L0_gnn_in['b2'], 'L1_gnn_basis1': _L1_gnn_in['basis1'], 'L1_gnn_att1': _L1_gnn_in['att1'], 'L1_gnn_gate_w1': _L1_gnn_in['gate_w1'], 'L1_gnn_root1': _L1_gnn_in['root1'], 'L1_gnn_bias1': _L1_gnn_in['bias1'], 'L1_gnn_basis2': _L1_gnn_in['basis2'], 'L1_gnn_att2': _L1_gnn_in['att2'], 'L1_gnn_gate_w2': _L1_gnn_in['gate_w2'], 'L1_gnn_root2': _L1_gnn_in['root2'], 'L1_gnn_bias2': _L1_gnn_in['bias2'], 'L2_gnn_W_qkv': _L2_gnn_in['W_qkv'], 'L2_gnn_b_qkv': _L2_gnn_in['b_qkv'], 'L2_gnn_W_ff': _L2_gnn_in['W_ff'], 'L2_gnn_b_ff': _L2_gnn_in['b_ff'], 'L3_gnn_W_l': _L3_gnn_in['W_l'], 'L3_gnn_W_r': _L3_gnn_in['W_r'], 'L3_gnn_b': _L3_gnn_in['b']}

def reference(x, src, dst, edge_type_2, edge_weight, L0_gnn_W1, L0_gnn_b1, L0_gnn_W2, L0_gnn_b2, L1_gnn_basis1, L1_gnn_att1, L1_gnn_gate_w1, L1_gnn_root1, L1_gnn_bias1, L1_gnn_basis2, L1_gnn_att2, L1_gnn_gate_w2, L1_gnn_root2, L1_gnn_bias2, L2_gnn_W_qkv, L2_gnn_b_qkv, L2_gnn_W_ff, L2_gnn_b_ff, L3_gnn_W_l, L3_gnn_W_r, L3_gnn_b):
    import jax
    import jax.numpy as jnp

    def _L0_gnn_ref(node_features, edge_index, edge_weight, W1, b1, W2, b2):
        import jax, jax.numpy as jnp
        import numpy as np
        EPS = 1e-12

        def _gcn_conv(x, W, b, src, dst, w, n_nodes):
            h = x @ W
            deg = jax.ops.segment_sum(w, dst, num_segments=n_nodes)
            dinv = jnp.where(deg > 0, jax.lax.rsqrt(deg), 0.0)
            norm = dinv[src] * w * dinv[dst]
            out = jax.ops.segment_sum(h[src] * norm[:, None], dst, num_segments=n_nodes)
            return out + b
        N = node_features.shape[0]
        loop = jnp.arange(N, dtype=edge_index.dtype)
        src = jnp.concatenate([edge_index[0], loop])
        dst = jnp.concatenate([edge_index[1], loop])
        w = jnp.concatenate([edge_weight, jnp.ones((N,), dtype=edge_weight.dtype)])
        x = _gcn_conv(node_features, W1, b1, src, dst, w, N)
        x = jax.nn.relu(x)
        x = _gcn_conv(x, W2, b2, src, dst, w, N)
        nrm = jnp.linalg.norm(x, axis=-1, keepdims=True)
        return x / jnp.maximum(nrm, EPS)

    def _L1_gnn_ref(x, edge_index, edge_type, basis1, att1, gate_w1, root1, bias1, basis2, att2, gate_w2, root2, bias2):
        import jax, jax.numpy as jnp
        import numpy as np
        NUM_RELATIONS = 2
        NUM_BASES = 30
        HIDDEN = 512
        N_NODES = 10000
        N_EDGES = 5000

        def rgcn_gate_layer(x, row, col, edge_type, basis, att, gate_w, root, bias):
            H = x.shape[1]
            w = jnp.einsum('rb,bio->rio', att, basis)
            x_j = x[col]
            msgs = []
            for r in range(NUM_RELATIONS):
                gate = jax.nn.sigmoid(x_j @ gate_w[r, :, 0])
                msgs.append(gate[:, None] * x_j @ w[r])
            msg = jnp.where((edge_type == 0)[:, None], msgs[0], msgs[1])
            agg = jax.ops.segment_sum(msg, row, num_segments=x.shape[0])
            return agg + x @ root + bias
        row, col = (edge_index[0], edge_index[1])
        h = jax.nn.relu(rgcn_gate_layer(x, row, col, edge_type, basis1, att1, gate_w1, root1, bias1))
        out = rgcn_gate_layer(h, row, col, edge_type, basis2, att2, gate_w2, root2, bias2)
        return out

    def _L2_gnn_ref(x, edge_index, W_qkv, b_qkv, W_ff, b_ff):
        import jax, jax.numpy as jnp
        import numpy as np
        from math import sqrt
        N = 50000
        E = 25000
        D_EMB = 512
        DK = 64
        DV = 64
        HEADS = 8

        def _attention_message(Q, K, V, senders, receivers, n_nodes):
            scale = 1.0 / sqrt(Q.shape[-1])
            scores = jnp.einsum('ehd,ehd->eh', Q[receivers], K[senders]) * scale
            smax = jax.ops.segment_max(scores, receivers, num_segments=n_nodes)
            ex = jnp.exp(scores - smax[receivers])
            denom = jax.ops.segment_sum(ex, receivers, num_segments=n_nodes)
            att = ex / denom[receivers]
            out = jax.ops.segment_sum(att[:, :, None] * V[senders], receivers, num_segments=n_nodes)
            return (out, att)
        n_nodes = x.shape[0]
        qkv = x @ W_qkv.T + b_qkv
        Q, K, V = jnp.split(qkv, [DK * HEADS, 2 * DK * HEADS], axis=-1)
        Q = Q.reshape(n_nodes, HEADS, DK)
        K = K.reshape(n_nodes, HEADS, DK)
        V = V.reshape(n_nodes, HEADS, DV)
        senders, receivers = (edge_index[0], edge_index[1])
        msg, _ = _attention_message(Q, K, V, senders, receivers, n_nodes)
        out = msg.reshape(n_nodes, HEADS * DV) @ W_ff.T + b_ff
        return out

    def _L3_gnn_ref(x, edge_index, W_l, W_r, b):
        import jax, jax.numpy as jnp
        import numpy as np
        N_NODES = 10000
        N_EDGES = 5000
        D_IN = 512
        D_OUT = 512
        src = edge_index[0]
        dst = edge_index[1]
        n = x.shape[0]
        msg = x[src]
        agg = jax.ops.segment_sum(msg, dst, num_segments=n)
        deg = jax.ops.segment_sum(jnp.ones((src.shape[0],), x.dtype), dst, num_segments=n)
        mean = agg / jnp.maximum(deg, 1.0)[:, None]
        h = mean @ W_l + b + x @ W_r
        return h * jax.nn.sigmoid(h)
    edge_index = jnp.stack([src, dst])
    x = _layernorm(x + _L0_gnn_ref(x, edge_index, edge_weight, L0_gnn_W1, L0_gnn_b1, L0_gnn_W2, L0_gnn_b2), axis=-1)
    x = _layernorm(x + _L1_gnn_ref(x, edge_index, edge_type_2, L1_gnn_basis1, L1_gnn_att1, L1_gnn_gate_w1, L1_gnn_root1, L1_gnn_bias1, L1_gnn_basis2, L1_gnn_att2, L1_gnn_gate_w2, L1_gnn_root2, L1_gnn_bias2), axis=-1)
    x = _layernorm(x + _L2_gnn_ref(x, edge_index, L2_gnn_W_qkv, L2_gnn_b_qkv, L2_gnn_W_ff, L2_gnn_b_ff), axis=-1)
    x = _layernorm(x + _L3_gnn_ref(x, edge_index, L3_gnn_W_l, L3_gnn_W_r, L3_gnn_b), axis=-1)
    return x

_drawn_inputs = setup_inputs


def setup_inputs(seed=0):
    import zlib

    import numpy as np

    out = dict(_drawn_inputs(seed))
    spreads = {'L0_gnn_b1': (0.0, 0.1),
     'L0_gnn_b2': (0.0, 0.1),
     'L2_gnn_b_qkv': (0.0, 0.1),
     'L2_gnn_b_ff': (0.0, 0.1),
     'L3_gnn_b': (0.0, 0.1)}
    factors = {'L1_gnn_basis1': 8.0,
     'L1_gnn_att1': 8.0,
     'L1_gnn_gate_w1': 30.108,
     'L1_gnn_root1': 8.0,
     'L1_gnn_bias1': 24.064,
     'L1_gnn_basis2': 8.0,
     'L1_gnn_att2': 8.0,
     'L1_gnn_gate_w2': 41.162,
     'L1_gnn_root2': 6.782,
     'L1_gnn_bias2': 8.0}
    for name, (base, spread) in spreads.items():
        noise = np.random.default_rng([zlib.crc32(name.encode()), seed]).standard_normal(out[name].shape)
        drawn = base * np.exp(spread * noise) if base else spread * noise
        out[name] = jnp.asarray(drawn.astype(out[name].dtype))
    for name, factor in factors.items():
        out[name] = (out[name] * factor).astype(out[name].dtype)
    return out
```

```python
import concourse.bass as bass
from concourse import mybir
from contextlib import ExitStack

F32, F32R, BF16, I32 = mybir.dt.float32, mybir.dt.float32r, mybir.dt.bfloat16, mybir.dt.int32
ALU, ACT, AX = mybir.AluOpType, mybir.ActivationFunctionType, mybir.AxisListType

N, EDGES, DM, DH = 10000, 5000, 512, 256
HEADS, DK = 8, 64
RELATIONS, BASES = 2, 30
NODE_COLS = -(-N // 128)
NODE_SPAN = NODE_COLS * 128
NODE_STEPS = NODE_COLS
ET, EP = 40, 125
D_TILES = -(-EDGES // 128)
S_TILES = D_TILES + 1
NO_ROW = 1 << 20
WIDE = S_TILES * 128 + 128


def prepare(nc, persist, src, dst, edge_type, edge_weight):
    P = persist
    tag = {"D": P.D, "S": P.S}
    pos_dram = {n: nc.dram_tensor(f"prep_node_{n}", [NODE_COLS * 128], F32).ap() for n in range(5)}
    seg_dram = {d: nc.dram_tensor(f"prep_ids_{d}", [tag[d].tiles * 128 + 1], F32).ap() for d in "DS"}

    ctx = ExitStack()
    with ctx:
        def sb(name, shape, dt=F32):
            return ctx.enter_context(nc.sbuf_tensor(name, shape, dt))

        def sem(name):
            return ctx.enter_context(nc.semaphore(name))

        raw_i = sb("raw_i", [ET, 3, EP], I32)
        raw_f = sb("raw_f", [ET, 4, EP])
        edge = sb("edge", [EP, 4, ET])
        edge_i = sb("edge_i", [EP, 2, ET], I32)
        part_i = sb("part_i", [EP, 2, ET], I32)
        lo = sb("lo", [EP, 2, ET])
        hi = sb("hi", [EP, 2, ET])
        key_bc = {d: sb(f"key_bc_{d}", [128, WIDE], I32) for d in "DS"}
        low_bc = sb("low_bc", [128, WIDE], I32)
        iota_i = sb("iota_i", [128, 2 * NODE_COLS], I32)
        iota = sb("iota", [128, 2 * NODE_COLS])
        iota_b = sb("iota_b", [128, 2 * NODE_COLS], BF16)
        lane_i = sb("lane_i", [128, 1], I32)
        lane = sb("lane", [128, 1])
        earlier = sb("earlier", [128, 128], BF16)
        below = sb("below", [128, 128])
        ones = sb("ones", [128, 128])
        oh_lo = {d: sb(f"oh_lo_{d}", [EP, ET, 128], BF16) for d in "DS"}
        oh_hi = {d: sb(f"oh_hi_{d}", [EP, ET, tag[d].cols], BF16) for d in "DS"}
        oh_loT = {d: sb(f"oh_loT_{d}", [128, EDGES], BF16) for d in "DS"}
        same = sb("same", [EP, ET, EP], BF16)
        in_tile = {d: sb(f"in_tile_{d}", [EP, ET]) for d in "DS"}
        found = {d: sb(f"found_{d}", [EP, ET]) for d in "DS"}
        junk = {d: sb(f"junk_{d}", [EP, tag[d].cols]) for d in "DS"}
        w_part = sb("w_part", [EP, 3, ET], BF16)
        w_rest = sb("w_rest", [EP, ET])
        total = {d: sb(f"total_{d}", [128, tag[d].cols]) for d in "DS"}
        runsum = {d: sb(f"runsum_{d}", [128, tag[d].cols]) for d in "DS"}
        start = {d: sb(f"start_{d}", [128, tag[d].cols]) for d in "DS"}
        table = {d: sb(f"table_{d}", [128, tag[d].cols]) for d in "DS"}
        table_hi = {d: sb(f"table_hi_{d}", [128, tag[d].cols], BF16) for d in "DS"}
        table_lo = {d: sb(f"table_lo_{d}", [128, tag[d].cols], BF16) for d in "DS"}
        pad_f = sb("pad_f", [128, 4])
        pad_i = sb("pad_i", [128, 4], I32)
        rank_i = sb("rank_i", [EP, ET], I32)
        rank_p = sb("rank_p", [EP, 2, ET], I32)
        rank_f = sb("rank_f", [EP, 2, ET])
        oh_pl = sb("oh_pl", [EP, ET, 128], BF16)
        oh_ph = sb("oh_ph", [EP, ET, 41], BF16)
        value = sb("value", [EP, 3, ET])
        v_part = sb("v_part", [EP, 3, 3, ET], BF16)
        sorted_f = {d: sb(f"sorted_{d}", [128, 3, 41]) for d in "DS"}
        node_f = sb("node_f", [128, 5, NODE_COLS])
        degree = sb("degree", [128, NODE_COLS])
        mask = sb("mask", [128, 2 * NODE_COLS])
        rowsT = sb("rowsT", [128, 5, 128])
        idsT = {d: sb(f"idsT_{d}", [41, 128]) for d in "DS"}
        col0 = sb("col0", [128, 5])
        minus7 = sb("minus7", [1, 1])
        minus_half = sb("minus_half", [128, NODE_COLS])
        ones_wide = sb("ones_wide", [128, 2 * NODE_COLS])
        wide = [key_bc["D"][0:EP, :].bitcast(BF16)[:, 0:ET * 123].rearrange("p (t a c) -> p t a c", a=3, c=41),
                key_bc["D"][0:EP, :].bitcast(BF16)[:, ET * 123:2 * ET * 123].rearrange("p (t a c) -> p t a c", a=3, c=41),
                key_bc["S"][0:EP, :].bitcast(BF16)[:, 0:ET * 123].rearrange("p (t a c) -> p t a c", a=3, c=41)]
        weighted = [key_bc["S"][0:EP, :].bitcast(BF16)[:, m * ET * NODE_COLS:(m + 1) * ET * NODE_COLS]
                    .rearrange("p (t c) -> p t c", c=NODE_COLS) for m in range(3)]
        ids_f = {"D": low_bc[:, :].bitcast(F32), "S": key_bc["D"][:, :].bitcast(F32)}

        ps_edge = ctx.enter_context(nc.psum_tensor("ps_edge", [128, 512], F32))
        ps_tot = {d: ctx.enter_context(nc.psum_tensor(f"ps_tot_{d}", [128, 512], F32)) for d in "DS"}
        ps_run = {d: ctx.enter_context(nc.psum_tensor(f"ps_run_{d}", [128, 512], F32)) for d in "DS"}
        ps_look = {d: ctx.enter_context(nc.psum_tensor(f"ps_look_{d}", [128, 512], F32)) for d in "DS"}
        ps_sort = ctx.enter_context(nc.psum_tensor("ps_sort", [128, 512], F32))

        raw_loaded, bc_loaded = sem("raw_loaded"), sem("bc_loaded")
        pool_made = sem("pool_made")
        dve_steps, pe_steps = sem("dve_steps"), sem("pe_steps")
        table_ready = {d: sem(f"table_ready_{d}") for d in "DS"}
        looked_up = {d: sem(f"looked_up_{d}") for d in "DS"}
        lookup_read = {d: sem(f"lookup_read_{d}") for d in "DS"}
        table_step = {d: sem(f"table_step_{d}") for d in "DS"}
        counted = {d: sem(f"counted_{d}") for d in "DS"}
        stored, reloaded, flags_loaded = sem("prep_stored"), sem("prep_reloaded"), sem("flags_loaded")
        mark = {}

        block = ctx.enter_context(nc.Block())

        @block.vector
        def _(dve):
            done = [0]

            def link(ins):
                done[0] += 1
                ins.then_inc(dve_steps, 1)
                dve.wait_ge(dve_steps, done[0])
                return done[0]

            def split(parts, rest, first):
                link(nc.vector.tensor_copy(parts[0], first))
                link(nc.vector.tensor_tensor(rest, first, parts[0], ALU.subtract))
                link(nc.vector.tensor_copy(parts[1], rest))
                return link(nc.vector.tensor_tensor(parts[2], rest, parts[1], ALU.subtract))

            link(nc.vector.memset(minus_half[:, :], -0.5))
            link(nc.vector.memset(ones_wide[:, :], 1.0))
            dve.wait_ge(pool_made, 6)
            link(nc.vector.tensor_copy(iota[:, :], iota_i[:, :]))
            link(nc.vector.tensor_copy(iota_b[:, :], iota_i[:, :]))
            link(nc.vector.tensor_copy(lane[:, :], lane_i[:, :]))
            link(nc.vector.tensor_scalar(earlier[:, :], iota[:, 0:128], lane[:, 0:1], None, ALU.is_lt))
            link(nc.vector.tensor_scalar(below[:, :], iota[:, 0:128], lane[:, 0:1], None, ALU.is_gt))
            dve.wait_ge(raw_loaded, 64)
            link(nc.vector.tensor_copy(raw_f[:, 0, :], raw_i[:, 1, :]))
            link(nc.vector.tensor_copy(raw_f[:, 3, :], raw_i[:, 0, :]))
            mark["raw rows"] = link(nc.vector.scalar_tensor_tensor(
                raw_f[:, 1, :], raw_i[:, 2, :], float(NODE_SPAN), raw_i[:, 0, :], ALU.mult, ALU.add))
            dve.wait_ge(pe_steps, 1)
            link(nc.vector.tensor_copy(edge[:, :, :], ps_edge[0:EP, 0:4 * ET].rearrange("p (a t) -> p a t", a=4)))
            link(nc.vector.tensor_copy(edge_i[:, :, :], edge[:, 0:2, :]))
            link(nc.vector.tensor_scalar(part_i[:, :, :], edge_i[:, :, :], 127, None, ALU.bitwise_and))
            link(nc.vector.tensor_copy(lo[:, :, :], part_i[:, :, :]))
            link(nc.vector.tensor_scalar(part_i[:, :, :], edge_i[:, :, :], 7, None, ALU.logical_shift_right))
            link(nc.vector.tensor_copy(hi[:, :, :], part_i[:, :, :]))
            split([w_part[:, n, :] for n in range(3)], w_rest[:, :], edge[:, 2, :])
            for n, d in enumerate("DS"):
                cols = tag[d].cols
                link(nc.vector.tensor_tensor(
                    oh_lo[d][:, :, :], iota[0:EP, 0:128].unsqueeze(1).broadcast_to([EP, ET, 128]),
                    lo[:, n, :].unsqueeze(2).broadcast_to([EP, ET, 128]), ALU.is_equal))
                mark["one-hots " + d] = link(nc.vector.tensor_tensor(
                    oh_hi[d][:, :, :], iota[0:EP, 0:cols].unsqueeze(1).broadcast_to([EP, ET, cols]),
                    hi[:, n, :].unsqueeze(2).broadcast_to([EP, ET, cols]), ALU.is_equal))
            dve.wait_ge(bc_loaded, 48)
            link(nc.vector.scalar_tensor_tensor(key_bc["S"][:, 0:EDGES], low_bc[:, 0:EDGES], float(NODE_SPAN), key_bc["S"][:, 0:EDGES],
                                                ALU.mult, ALU.add))
            for n, d in enumerate("DS"):
                link(nc.vector.tensor_scalar(low_bc[:, 0:EDGES], key_bc[d][:, 0:EDGES], 127, None, ALU.bitwise_and))
                mark["lookup one-hots " + d] = link(nc.vector.tensor_scalar(
                    oh_loT[d][:, :], low_bc[:, 0:EDGES], lane[:, 0:1], None, ALU.is_equal))
                link(nc.vector.tensor_tensor(
                    same[:, :, :], key_bc[d][0:EP, 0:EDGES].rearrange("p (t q) -> p t q", q=EP),
                    edge[:, n, :].unsqueeze(2).broadcast_to([EP, ET, EP]), ALU.is_equal))
                link(nc.vector.tensor_tensor(same[:, :, :], same[:, :, :],
                                             earlier[0:EP, 0:EP].unsqueeze(1).broadcast_to([EP, ET, EP]), ALU.mult))
                link(nc.vector.reduce_sum(in_tile[d][:, :], same[:, :, :], AX.X))

            dve.wait_ge(pe_steps, 3)
            for d in "DS":
                cols = tag[d].cols
                link(nc.vector.tensor_copy(total[d][:, :], ps_tot[d][:, 0:cols]))
                link(nc.vector.tensor_tensor_scan(runsum[d][:, :], ones_wide[:, 0:cols], total[d][:, :], 0.0,
                                                  ALU.mult, ALU.add))
                mark["prefix " + d] = link(nc.vector.tensor_tensor(
                    runsum[d][:, :], runsum[d][:, :], total[d][:, :], ALU.subtract))
            dve.wait_ge(pe_steps, 5)
            link(nc.vector.tensor_copy(start["D"][:, :], ps_tot["D"][:, 0:NODE_COLS]))
            link(nc.vector.tensor_copy(start["S"][:, :], ps_tot["S"][:, 0:2 * NODE_COLS]))
            link(nc.vector.tensor_copy(pad_i[:, 0:1], ps_sort[:, 0:1]))
            link(nc.vector.tensor_scalar(pad_f[:, 0:1], ps_sort[:, 0:1], -1.0, None, ALU.mult))
            link(nc.vector.tensor_copy(pad_i[:, 1:2], pad_f[:, 0:1]))
            link(nc.vector.tensor_scalar(pad_i[:, 2:3], pad_i[:, 1:2], 127, None, ALU.bitwise_and))
            link(nc.vector.tensor_copy(pad_f[:, 1:2], pad_i[:, 2:3]))
            link(nc.vector.tensor_tensor(pad_f[:, 2:3], pad_f[:, 1:2], ps_sort[:, 0:1], ALU.add))
            link(nc.vector.tensor_scalar(pad_f[:, 3:4], pad_f[:, 2:3], 1.0 / 128, None, ALU.mult))
            link(nc.vector.tensor_copy(P.type0_tiles[:, :], pad_f[:, 3:4]))
            link(nc.vector.tensor_scalar(P.is_type0[:, :], iota[:, 0:P.S.tiles], pad_f[:, 3:4], None, ALU.is_lt))
            link(nc.vector.tensor_scalar(start["S"][:, NODE_COLS:], start["S"][:, NODE_COLS:], pad_f[:, 1:2],
                                         None, ALU.add))

            def advance(d, t, first):
                cols = tag[d].cols
                if first:
                    nc.vector.tensor_copy(table[d][:, :], start[d][:, :]).then_inc(table_step[d], 1)
                else:
                    dve.wait_ge(counted[d], t)
                    nc.vector.tensor_tensor(table[d][:, :], ps_run[d][:, 0:cols], start[d][:, :], ALU.add)\
                        .then_inc(table_step[d], 1)

            def halve(d, t, first):
                if not first:
                    dve.wait_ge(looked_up[d], t)
                dve.wait_ge(table_step[d], 2 * t + 1)
                nc.vector.tensor_copy(table_hi[d][:, :], table[d][:, :]).then_inc(table_step[d], 1)

            def rest(d, t):
                dve.wait_ge(table_step[d], 2 * t + 2)
                nc.vector.tensor_tensor(table_lo[d][:, :], table[d][:, :], table_hi[d][:, :], ALU.subtract)\
                    .then_inc(table_ready[d], 1)

            def pick(d, t):
                dve.wait_ge(looked_up[d], t + 1)
                if not isinstance(t, int) or t > 0:
                    dve.wait_ge(lookup_read[d], t)
                nc.vector.scalar_tensor_tensor(
                    junk[d][:, :], ps_look[d][0:EP, 0:tag[d].cols], 1.0,
                    oh_hi[d][:, bass.ds(t, 1), :].rearrange("p a c -> p (a c)"), ALU.mult, ALU.mult,
                    accum_out=found[d][:, bass.ds(t, 1)]).then_inc(lookup_read[d], 1)

            def place(t, first):
                for d in "DS":
                    advance(d, t, first)
                for d in "DS":
                    halve(d, t, first)
                for d in "DS":
                    rest(d, t)
                for d in "DS":
                    pick(d, t)

            place(0, True)
            with dve.Fori(1, ET) as t:
                place(t, False)
            dve.wait_ge(lookup_read["D"], ET)
            dve.wait_ge(lookup_read["S"], ET)

            for d in "DS":
                cols = tag[d].cols
                link(nc.vector.tensor_tensor(rank_i[:, :], found[d][:, :], in_tile[d][:, :], ALU.add))
                link(nc.vector.tensor_scalar(rank_p[:, 0, :], rank_i[:, :], 127, None, ALU.bitwise_and))
                link(nc.vector.tensor_scalar(rank_p[:, 1, :], rank_i[:, :], 7, None, ALU.logical_shift_right))
                link(nc.vector.tensor_copy(rank_f[:, :, :], rank_p[:, :, :]))
                if d == "S":
                    dve.wait_ge(pe_steps, 6)
                link(nc.vector.tensor_tensor(
                    oh_pl[:, :, :], iota[0:EP, 0:128].unsqueeze(1).broadcast_to([EP, ET, 128]),
                    rank_f[:, 0, :].unsqueeze(2).broadcast_to([EP, ET, 128]), ALU.is_equal))
                link(nc.vector.tensor_tensor(
                    oh_ph[:, :, :], iota[0:EP, 0:41].unsqueeze(1).broadcast_to([EP, ET, 41]),
                    rank_f[:, 1, :].unsqueeze(2).broadcast_to([EP, ET, 41]), ALU.is_equal))
                link(nc.vector.tensor_scalar(value[:, 0, :], edge[:, 0 if d == "D" else 1, :], 1.0, None, ALU.add))
                link(nc.vector.tensor_scalar(value[:, 1, :], edge[:, 3 if d == "D" else 0, :], 1.0, None, ALU.add))
                link(nc.vector.tensor_copy(value[:, 2, :], edge[:, 2, :]))
                for n in range(3):
                    split([v_part[:, m, n, :] for m in range(3)], w_rest[:, :], value[:, n, :])
                for m in range(3):
                    for n in range(3):
                        step = link(nc.vector.tensor_tensor(
                            wide[m][:, :, n, :], oh_ph[:, :, :],
                            v_part[:, m, n, :].unsqueeze(2).broadcast_to([EP, ET, 41]), ALU.mult))
                mark["ordering operands " + d] = step
                dve.wait_ge(pe_steps, 6 if d == "D" else 7)
                link(nc.vector.tensor_copy(sorted_f[d][:, :, :],
                                           ps_sort[:, 0:123].rearrange("p (a c) -> p a c", a=3)))
                tiles = tag[d].tiles
                link(nc.vector.tensor_scalar(tag[d].gather[:, :], sorted_f[d][:, 1, 0:tiles], -1.0, 0.0,
                                             ALU.add, ALU.max))
                if d == "D":
                    link(nc.vector.tensor_scalar(P.receivers[:, :], sorted_f[d][:, 0, 0:tiles], -1.0, 0.0,
                                                 ALU.add, ALU.max))
                    link(nc.vector.tensor_copy(P.weights[:, :], sorted_f[d][:, 2, 0:tiles]))
                mark["sorted " + d] = done[0]

            for m in range(3):
                mark["weighted one-hots"] = link(nc.vector.tensor_tensor(
                    weighted[m], oh_hi["D"][:, :, :], w_part[:, m, :].unsqueeze(2).broadcast_to([EP, ET, NODE_COLS]),
                    ALU.mult))

            for d, rows in (("D", [0]), ("S", [1, 2])):
                cols = tag[d].cols
                link(nc.vector.tensor_scalar(mask[:, 0:cols], total[d][:, :], 0.0, float(NO_ROW), ALU.is_equal, ALU.mult))
                link(nc.vector.scalar_tensor_tensor(table["S"][:, 0:cols], total[d][:, :], -1.0, start[d][:, :],
                                                    ALU.add, ALU.add))
                link(nc.vector.tensor_tensor(
                    node_f[:, rows[0]:rows[-1] + 1, :].rearrange("p a c -> p (a c)"), table["S"][:, 0:cols],
                    mask[:, 0:cols], ALU.add))
            dve.wait_ge(pe_steps, 8)
            link(nc.vector.tensor_scalar(degree[:, :], ps_edge[:, 0:NODE_COLS], 1.0, None, ALU.add))
            link(nc.vector.tensor_scalar(mask[:, 0:NODE_COLS], degree[:, :], 0.0, None, ALU.is_gt))
            mark["degree clamped"] = link(nc.vector.tensor_scalar(degree[:, :], degree[:, :], 1e-30, None, ALU.max))
            dve.wait_ge(pool_made, 7)
            link(nc.vector.tensor_tensor(node_f[:, 3, :], degree[:, :], mask[:, 0:NODE_COLS], ALU.mult))
            link(nc.vector.tensor_scalar(mask[:, 0:NODE_COLS], total["D"][:, :], 1.0, None, ALU.max))
            mark["node tables"] = link(nc.vector.reciprocal(node_f[:, 4, :], mask[:, 0:NODE_COLS]))
            dve.wait_ge(pe_steps, 9)
            link(nc.vector.tensor_copy(rowsT[0:NODE_COLS, :, :].rearrange("p a c -> p (a c)")[:, 0:512],
                                       ps_tot["D"][0:NODE_COLS, :]))
            link(nc.vector.tensor_copy(rowsT[0:NODE_COLS, 4, :], ps_tot["S"][0:NODE_COLS, 0:128]))
            link(nc.vector.tensor_copy(idsT["D"][0:40, :], ps_tot["S"][0:40, 128:256]))
            mark["transposed"] = link(nc.vector.tensor_copy(idsT["S"][:, :], ps_tot["S"][0:41, 256:384]))
            dve.wait_ge(reloaded, 80)
            for n, out in enumerate((P.last_D, P.last_S0, P.last_S1, P.dinv, P.rdeg)):
                link(nc.vector.tensor_copy(out[:, 0:1], col0[:, n:n + 1]))
                link(nc.vector.tensor_copy(out[:, 1:NODE_STEPS], node_f[:, n, 0:NODE_STEPS - 1]))
            for d in "DS":
                m = tag[d].tiles * 128
                dve.wait_ge(flags_loaded, 32)
                ids = ids_f[d]
                link(nc.vector.tensor_tensor(tag[d].same_run[:, 0:m], ids[:, 1:m + 1], ids[:, 0:m], ALU.is_equal))
                link(nc.vector.memset(tag[d].same_run[:, m:m + 1], 0.0))

        @block.gpsimd
        def _(pool):
            nc.gpsimd.iota(iota_i[:, :], pattern=[[1, 2 * NODE_COLS]], base=0, channel_multiplier=0).then_inc(pool_made, 1)
            nc.gpsimd.iota(lane_i[:, :], pattern=[[0, 1]], base=0, channel_multiplier=1).then_inc(pool_made, 1)
            nc.gpsimd.memset(ones[:, :], 1.0).then_inc(pool_made, 1)
            nc.gpsimd.memset(minus7[:, :], -7.0).then_inc(pool_made, 1)
            nc.gpsimd.memset(P.ident[:, :], 0.0).then_inc(pool_made, 1)
            pool.wait_ge(pool_made, 5)
            nc.gpsimd.affine_select(out=P.ident[:, :], in_=P.ident[:, :], compare_op=ALU.not_equal, fill=1.0,
                                    base=0, pattern=[[-1, 128]], channel_multiplier=1).then_inc(pool_made, 1)
            pool.wait_ge(dve_steps, mark["degree clamped"])
            nc.gpsimd.tensor_tensor(degree[:, :], degree[:, :], minus_half[:, :], ALU.pow).then_inc(pool_made, 1)

        @block.tensor
        def _(pe):
            pe.wait_ge(dve_steps, mark["raw rows"])
            for n in range(4):
                last = nc.tensor.transpose(ps_edge[0:EP, n * ET:(n + 1) * ET], raw_f[:, n, :], P.ident[0:ET, 0:ET])
            last.then_inc(pe_steps, 1)
            for d in "DS":
                cols = tag[d].cols
                pe.wait_ge(dve_steps, mark["one-hots " + d])

                def count(t, **flags):
                    return nc.tensor.matmul(ps_tot[d][:, 0:cols], oh_lo[d][:, bass.ds(t, 1), :].rearrange("p a c -> p (a c)"),
                                            oh_hi[d][:, bass.ds(t, 1), :].rearrange("p a c -> p (a c)"),
                                            skip_group_check=True, **flags)
                count(0, start=True, stop=False)
                with pe.Fori(1, ET - 1) as t:
                    count(t, start=False, stop=False)
                count(ET - 1, start=False, stop=True).then_inc(pe_steps, 1)
            for d in "DS":
                cols = tag[d].cols
                pe.wait_ge(dve_steps, mark["prefix S"])
                nc.tensor.matmul(ps_tot[d][:, 0:cols], below[:, :], total[d][:, :], start=True, stop=False)
                last = nc.tensor.matmul(ps_tot[d][:, 0:cols], ones[:, :], runsum[d][:, :], start=False, stop=True)
                if d == "D":
                    last.then_inc(pe_steps, 1)
            nc.tensor.matmul(ps_sort[:, 0:1], ones[:, :], runsum["S"][:, NODE_COLS:NODE_COLS + 1], start=True, stop=True)\
                .then_inc(pe_steps, 1)

            def look_up(d, t, first):
                if not first:
                    pe.wait_ge(lookup_read[d], t)
                pe.wait_ge(table_ready[d], t + 1)
                cols = tag[d].cols
                one_hot = oh_loT[d][:, bass.ds(t * EP, EP)]
                nc.tensor.matmul(ps_look[d][0:EP, 0:cols], one_hot, table_hi[d][:, :], start=True, stop=False)
                nc.tensor.matmul(ps_look[d][0:EP, 0:cols], one_hot, table_lo[d][:, :], start=False, stop=True)\
                    .then_inc(looked_up[d], 1)

            def count_on(d, t, first):
                nc.tensor.matmul(ps_run[d][:, 0:tag[d].cols], oh_lo[d][:, bass.ds(t, 1), :].rearrange("p a c -> p (a c)"),
                                 oh_hi[d][:, bass.ds(t, 1), :].rearrange("p a c -> p (a c)"),
                                 start=first, stop=True, skip_group_check=True).then_inc(counted[d], 1)

            for d in "DS":
                look_up(d, 0, True)
                count_on(d, 0, True)
            with pe.Fori(1, ET) as t:
                for d in "DS":
                    look_up(d, t, False)
                    count_on(d, t, False)

            for d in "DS":
                pe.wait_ge(dve_steps, mark["ordering operands " + d])
                if d == "S":
                    pe.wait_ge(dve_steps, mark["sorted D"])

                def order(t, begin, end):
                    for m in range(3):
                        last = nc.tensor.matmul(ps_sort[:, 0:123], oh_pl[:, bass.ds(t, 1), :].rearrange("p a c -> p (a c)"),
                                                wide[m][:, bass.ds(t, 1), :, :].rearrange("p b a c -> p (b a c)"),
                                                start=begin and m == 0, stop=end and m == 2, skip_group_check=True)
                    return last
                order(0, True, False)
                with pe.Fori(1, ET - 1) as t:
                    order(t, False, False)
                order(ET - 1, False, True).then_inc(pe_steps, 1)
            pe.wait_ge(dve_steps, mark["weighted one-hots"])

            def weigh(t, begin, end):
                for m in range(3):
                    last = nc.tensor.matmul(ps_edge[:, 0:NODE_COLS], oh_lo["D"][:, bass.ds(t, 1), :].rearrange("p a c -> p (a c)"),
                                            weighted[m][:, bass.ds(t, 1), :].rearrange("p a c -> p (a c)"),
                                            start=begin and m == 0, stop=end and m == 2, skip_group_check=True)
                return last
            weigh(0, True, False)
            with pe.Fori(1, ET - 1) as t:
                weigh(t, False, False)
            weigh(ET - 1, False, True).then_inc(pe_steps, 1)
            pe.wait_ge(dve_steps, mark["node tables"])
            for n in range(5):
                out = ps_tot["D"][0:NODE_COLS, n * 128:(n + 1) * 128] if n < 4 else ps_tot["S"][0:NODE_COLS, 0:128]
                nc.tensor.transpose(out, node_f[:, n, :], P.ident[:, :])
            nc.tensor.transpose(ps_tot["S"][0:40, 128:256], sorted_f["D"][:, 0, 0:40], P.ident[:, :])
            nc.tensor.transpose(ps_tot["S"][0:41, 256:384], sorted_f["S"][:, 0, 0:41], P.ident[:, :]).then_inc(pe_steps, 1)

        @block.sync
        def _(sp):
            for n, a in enumerate((src, dst, edge_type)):
                sp.dma_start(raw_i[:, n, :], a.rearrange("(t p) -> t p", p=EP)).then_inc(raw_loaded, 16)
            sp.dma_start(raw_f[:, 2, :], edge_weight.rearrange("(t p) -> t p", p=EP)).then_inc(raw_loaded, 16)
            for a, out in ((dst, key_bc["D"]), (src, key_bc["S"]), (edge_type, low_bc)):
                sp.dma_start(out[:, 0:EDGES], a.partition_broadcast(128)).then_inc(bc_loaded, 16)
            sp.wait_ge(dve_steps, mark["transposed"])
            for n in range(5):
                sp.dma_start(pos_dram[n].rearrange("(h l) -> h l", l=128), rowsT[0:NODE_COLS, n, :]).then_inc(stored, 16)
            for d in "DS":
                sp.dma_start(seg_dram[d][1:].rearrange("(h l) -> h l", l=128), idsT[d][0:tag[d].tiles, :])\
                    .then_inc(stored, 16)
                sp.dma_start(seg_dram[d][0:1].rearrange("(a n) -> a n", a=1), minus7[:, :]).then_inc(stored, 16)
            sp.wait_ge(stored, 9 * 16)
            for n in range(5):
                sp.dma_start(col0[:, n:n + 1], pos_dram[n][N - 128:N].rearrange("(p a) -> p a", a=1)).then_inc(reloaded, 16)
            for d in "DS":
                m = tag[d].tiles * 128 + 1
                sp.dma_start(ids_f[d][:, 0:m], seg_dram[d].partition_broadcast(128)).then_inc(flags_loaded, 16)



def combine_bases(nc, mixed_w, all_att, all_basis):
    QUARTERS = 4
    K = BASES * QUARTERS
    WIDTH = DM // QUARTERS * DM
    CHUNK = 4096
    CHUNKS = WIDTH // CHUNK
    GROUPS = CHUNK // 2048
    ctx = ExitStack()
    with ctx:
        bases = ctx.enter_context(nc.sbuf_tensor("bases", [K, 4, CHUNK], F32))
        mixed = ctx.enter_context(nc.sbuf_tensor("mixed", [128, 2, 4 * GROUPS, 512], F32))
        att = [ctx.enter_context(nc.sbuf_tensor(f"att_{l}", [K, 32], F32)) for l in range(2)]
        ps = ctx.enter_context(nc.psum_tensor("ps_mix", [128, 4, 512], F32))
        att_zeroed, att_loaded = (ctx.enter_context(nc.semaphore(n)) for n in ("att_zeroed", "att_loaded"))
        bases_loaded = [ctx.enter_context(nc.semaphore(f"bases_loaded{s}")) for s in range(4)]
        mixed_done, copied_act, copied_dve = (ctx.enter_context(nc.semaphore(n))
                                              for n in ("mix_done", "mix_copied_act", "mix_copied_dve"))
        mix_stored = [ctx.enter_context(nc.semaphore(f"mix_stored{s}")) for s in range(2)]
        QUADS = CHUNKS // 4
        block = ctx.enter_context(nc.Block())

        @block.vector
        def _(dve):
            for a in att:
                nc.vector.memset(a[:, :], 0.0).then_inc(att_zeroed, 1)

            for l in range(2):
                for q in range(QUADS):
                    for c in range(4):
                        g = 4 * (l * QUADS + q) + c
                        dve.wait_ge(mixed_done, 2 * g + 2)
                        if l * QUADS + q >= 2:
                            dve.wait_ge(mix_stored[(l * QUADS + q) % 2], 64 * ((l * QUADS + q) // 2))
                        nc.vector.tensor_copy(mixed[:, (l * QUADS + q) % 2, 2 * c + 1, :], ps[:, (2 * c + 1) % 4, :])\
                            .then_inc(copied_dve, 1)

        @block.scalar
        def _(act):
            for l in range(2):
                for q in range(QUADS):
                    for c in range(4):
                        g = 4 * (l * QUADS + q) + c
                        act.wait_ge(mixed_done, 2 * g + 1)
                        if l * QUADS + q >= 2:
                            act.wait_ge(mix_stored[(l * QUADS + q) % 2], 64 * ((l * QUADS + q) // 2))
                        nc.scalar.activation(mixed[:, (l * QUADS + q) % 2, 2 * c, :], ps[:, 2 * c % 4, :], ACT.Copy)\
                            .then_inc(copied_act, 1)
                    act.wait_ge(copied_act, 4 * (l * QUADS + q + 1))
                    act.wait_ge(copied_dve, 4 * (l * QUADS + q + 1))
                    for j in range(4):
                        out = mixed_w[l].rearrange("m (q g j n) -> m q g j n", q=QUADS, j=4, n=512)[:, q, :, j, :]
                        act.dma_start(out, mixed[32 * j:32 * j + RELATIONS * QUARTERS, (l * QUADS + q) % 2, :, :])\
                            .then_inc(mix_stored[(l * QUADS + q) % 2], 16)
            for stored in mix_stored:
                act.wait_ge(stored, 64 * QUADS)

        @block.tensor
        def _(pe):
            pe.wait_ge(att_loaded, 2 * QUARTERS * RELATIONS * 16)

            for l in range(2):
                for q in range(QUADS):
                    for c in range(4):
                        g = 4 * (l * QUADS + q) + c
                        pe.wait_ge(bases_loaded[c], 16 * (l * QUADS + q + 1))
                        for h in range(GROUPS):
                            if g >= 2:
                                pe.wait_ge(copied_act if h == 0 else copied_dve, g - 1)
                            for j in range(4):
                                col = (4 * h + j) * 512
                                last = nc.tensor.matmul(ps[32 * j:32 * j + 32, (2 * c + h) % 4, :], att[l][:, :],
                                                        bases[:, c, col:col + 512], start=True, stop=True)
                            last.then_inc(mixed_done, 1)

        @block.sync
        def _(sp):
            sp.wait_ge(att_zeroed, 2)
            with nc.allow_non_contiguous_dma(reason="60 coefficients"):
                for l in range(2):
                    for s in range(QUARTERS):
                        for r in range(RELATIONS):
                            col = QUARTERS * r + s
                            sp.dma_start(att[l][s:K:QUARTERS, col:col + 1],
                                         all_att[l][r:r + 1, :].rearrange("a b -> b a")).then_inc(att_loaded, 16)
            for l in range(2):
                view = all_basis[l].rearrange("b (s i) o -> (b s) (i o)", s=QUARTERS)
                for q in range(QUADS):
                    for c in range(4):
                        g = 4 * q + c
                        if l * QUADS + q >= 1:
                            sp.wait_ge(mixed_done, 2 * (4 * (l * QUADS + q - 1) + c + 1))
                        sp.dma_start(bases[:, c, :], view[:, g * CHUNK:(g + 1) * CHUNK]).then_inc(bases_loaded[c], 16)


class Named:
    pass


class Ordering:

    def __init__(self, tiles, cols, gather, same_run):
        self.tiles, self.cols, self.gather, self.same_run = tiles, cols, gather, same_run


class Step:

    def __init__(self, c, i=None):
        self.c, self.i = c, i

    def number(self, first=0, each=1):
        return first + each * self.c if self.i is None else first + each * self.c + 4 * each * self.i

    def quarter(self, first, each=16):
        k = (first + self.c) // 4 + 1
        return each * k if self.i is None else each * k + each * self.i

    @property
    def t(self):
        return self.number()

    def back(self, k):
        return Step(self.c - k, self.i)


def pipelined(eng, n, *stages):
    lag = max(l for l, _ in stages)
    head = lag + 4 + (n - lag) % 4
    for j in range(head):
        for l, stage in stages:
            if j >= l:
                stage(Step(j - l))
    with eng.Fori(0, (n - head) // 4) as i:
        for s in range(4):
            for l, stage in stages:
                stage(Step(head + s - l, i))
    for j in range(n, n + lag):
        for l, stage in stages:
            if j - l < n:
                stage(Step(j - l))


PASSES = {"N1": NODE_STEPS, "E1": D_TILES, "N2": NODE_STEPS, "E2": D_TILES, "N3": NODE_STEPS,
          "E3": S_TILES, "N4": NODE_STEPS, "E4": S_TILES, "N5": NODE_STEPS, "E5": D_TILES,
          "E6": D_TILES, "N6": NODE_STEPS, "E7": D_TILES, "N7": NODE_STEPS}
DENSE = ("N1", "N3", "E3", "N4", "E4", "N5", "E5", "E6", "E7", "N7")
TRANSPOSED = ("N1", "E1", "E2", "N3", "E3", "N4", "E4", "N5", "E5", "E6", "E7", "N7")
SCANNED = ("E1", "E2", "E3", "E4", "E6", "E7")
GATHERS = ("N2", "N3", "N4", "N5", "N6", "N7")
GATHERED = ("E1", "E2", "E3", "E4", "E5", "E7")
LOADED = tuple(p for p in PASSES if p not in GATHERED)
LISTED = ("N2", "N4")
RESIDUAL = {"N3": 0, "N5": 0, "N7": 2}
NORMED = ("N3", "N5", "N6", "N7")


class Tally:

    def __init__(self, sem, passes, credit=0):
        self.sem, self.credit, self.first, self.last, at = sem, credit, {}, {}, 0
        for p, n in PASSES.items():
            self.first[p] = at
            at += n if p in passes else 0
            self.last[p] = at

    def done(self, p, step):
        return self.sem, step.number(self.credit + self.first[p] + 1)

    def free(self, p, step, depth):
        return self.sem, step.number(self.credit + self.first[p] + 1 - depth)

    def through(self, p):
        return self.sem, self.credit + self.last[p]


class Ring:

    def __init__(self, sems, passes, credit=0):
        self.sems, self.credit, self.first, at = sems, credit, {}, 0
        for p, n in PASSES.items():
            self.first[p] = at
            at += n if p in passes else 0
        self.passes, self.total = passes, at

    def slot(self, p, step):
        return (self.first[p] + step.c) % 4

    def sem(self, p, step):
        return self.sems[self.slot(p, step)]

    def done(self, p, step):
        return self.sem(p, step), step.quarter(self.first[p])

    def free(self, p, step):
        return self.sem(p, step), step.quarter(self.first[p])

    def through(self, p):
        n = self.first[p] + (PASSES[p] if p in self.passes else 0)
        return [(self.sems[s], self.credit + 16 * len(range(s, n, 4))) for s in range(4)]


def layers_block(nc, P, x, out, par, drams):
    X = drams
    ctx = ExitStack()
    with ctx:
        def sb(name, shape, dt=F32):
            return ctx.enter_context(nc.sbuf_tensor(name, shape, dt))

        def sem(name):
            return ctx.enter_context(nc.semaphore(name))

        rows = sb("rows", [128, 5, 4, DM])
        xin, agg, agg2, res, outs = (rows[:, n, :, :] for n in range(5))
        y = sb("y", [128, 4, DM])
        scan = sb("scan", [128, 2, DM])
        xT_hi, xT_lo = sb("xT_hi", [128, 2, DM], F32R), sb("xT_lo", [128, 2, DM], F32R)
        rT_hi, rT_lo = sb("rT_hi", [128, 2, DM], F32R), sb("rT_lo", [128, 2, DM], F32R)
        we_hi, we_lo = sb("we_hi", [128, 3, 4, DM], F32R), sb("we_lo", [128, 3, 4, DM], F32R)
        wn_hi, wn_lo = sb("wn_hi", [128, 4, DM], F32R), sb("wn_lo", [128, 4, DM], F32R)
        staged = sb("staged", [128, 4 * DM])
        b1 = sb("b1", [128, DH])
        b2, bias1, bias2, bff, b3 = (sb(n, [128, DM]) for n in ("b2", "bias1", "bias2", "bff", "b3"))
        bqkv = sb("bqkv", [128, 3, DM])
        gate = sb("gate", [128, RELATIONS, DM])
        prod = sb("prod", [128, DM])
        srow = sb("srow", [HEADS, D_TILES * 128])
        scores = sb("scores", [128, 2, HEADS])
        att = sb("att", [HEADS, 2, 128])
        list_col = [sb(f"list_col{n}", [128, 4], I32) for n in range(2)]
        z = sb("z", [128, 4])
        g = sb("g", [128, 4])
        sq = sb("sq", [128, 4])
        rn = sb("rn", [128, 4])
        stats = sb("stats", [128, 4, 6])
        mv = sb("mv", [128, 4, 2])
        ve = sb("ve", [128, 4])
        zero = sb("zero", [128, 1])
        half = sb("half", [128, 1])
        rstd = sb("rstd", [128, 4])
        nb = sb("nb", [128, 4])
        pT = ctx.enter_context(nc.psum_tensor("pT", [128, 2, DM], F32))
        pM = ctx.enter_context(nc.psum_tensor("pM", [128, 6, DM], F32))

        loaded = Ring([sem(f"loaded{s}") for s in range(4)], LOADED)
        gathered = Ring([sem(f"gathered{s}") for s in range(4)], GATHERED)
        agg_in = Ring([sem(f"agg_in{s}") for s in range(4)], GATHERS + ("E5",))
        agg2_in = Ring([sem(f"agg2_in{s}") for s in range(4)], ("N4", "N5"))
        res_in = Ring([sem(f"res_in{s}") for s in range(4)], RESIDUAL)
        stored = Ring([sem(f"stored{s}") for s in range(4)], PASSES, credit=16)
        list_copied = Tally(sem("list_copied"), [p for p in GATHERS + GATHERED if p not in LISTED])
        list_copied2 = Tally(sem("list_copied2"), ("N5", "E5"))
        listed = Tally(sem("listed"), LISTED)
        listed2 = Tally(sem("listed2"), ("N4",))
        prefilled = Tally(sem("prefilled"), ("N3", "N7"))
        prefilled2 = Tally(sem("prefilled2"), ("N5",))
        bias_filled = Tally(sem("bias_filled"), ("N5", "N6"))
        transposed = Tally(sem("transposed"), TRANSPOSED)
        high = Tally(sem("high"), DENSE)
        split = Tally(sem("split"), DENSE)
        scanned = Tally(sem("scanned"), SCANNED)
        scaled = Tally(sem("scaled"), ("E1", "E2", "E3", "E4", "E6"))
        gated = Tally(sem("gated"), ("E3", "E4"))
        sigmoid = Tally(sem("sigmoid"), ("E3", "E4"))
        summed = Tally(sem("summed"), ("N2", "N3", "N6"))
        product = Tally(sem("product"), TRANSPOSED, credit=2)
        evacuated = Tally(sem("evacuated"), [p for p in TRANSPOSED if p != "E5"], credit=2)
        added = Tally(sem("added"), ("N2", "N4", "N5"))
        squared = Tally(sem("squared"), ("N3",))
        bounded = Tally(sem("bounded"), ("N3",))
        inv_norm = Tally(sem("inv_norm"), ("N3",))
        silued = Tally(sem("silued"), ("N7",))
        biased = Tally(sem("biased"), ("N7",))
        y_ready = Tally(sem("y_ready"), ("N3", "N5", "N7"))
        bn_done = Tally(sem("bn_done"), NORMED)
        mean_ready = Tally(sem("mean_ready"), NORMED)
        var_ready = Tally(sem("var_ready"), NORMED)
        rstd_ready = Tally(sem("rstd_ready"), NORMED)
        shift_ready = Tally(sem("shift_ready"), NORMED)
        finished = Tally(sem("finished"), ("N2", "N3", "N4", "N5", "N6", "N7"), credit=4)
        scored = Tally(sem("scored"), ("E5",))
        score_T = Tally(sem("score_T"), ("E5",))
        score_kept = Tally(sem("score_kept"), ("E5",))
        qk_added = Tally(sem("qk_added"), ("E5",))
        v_done = Tally(sem("v_done"), ("E5",))
        v_added = Tally(sem("v_added"), ("E5",))
        multiplied = Tally(sem("multiplied"), ("E5",))
        att_cut = Tally(sem("att_cut"), ("E6",))
        att_T = Tally(sem("att_T"), ("E6",))
        softmax = sem("softmax")
        exps = sem("exps")
        w_loaded, w_high, w_low = sem("w_loaded"), sem("w_high"), sem("w_low")
        consts_loaded, half_set, zero_set = sem("consts_loaded"), sem("half_set"), sem("zero_set")
        settled = sem("settled")

        def wait(eng, pair):
            eng.wait_ge(pair[0], pair[1])

        def wait_all(eng, pairs):
            for pair in pairs:
                wait(eng, pair)

        def xin_in(p):
            return loaded if p in LOADED else gathered

        def settle(eng):
            eng.sem_inc(settled, 1)

        def col(table, step):
            return table[:, bass.ds(step.t, 1)]

        def node_rows(array, step):
            return array[N - 128:N, :] if step.i is None and step.c == 0 else \
                array[bass.ds(step.number(-128, 128), 128), :]

        def edge_rows(array, step):
            return array[bass.ds(step.number(0, 128), 128), :]

        def halves(place):
            return (wn_hi[:, :, :], wn_lo[:, :, :]) if place == "n" else (we_hi[:, place, :, :], we_lo[:, place, :, :])

        def square(a):
            return a.rearrange("(k p) n -> p k n", p=128)

        def relation(l, r):
            return X.mixed[l].rearrange("(r s) (i o) -> r i s o", r=RELATIONS, o=DM)[r]

        WEIGHTS = [("N1", "n", square(par.W1), DM // 128, DH, None),
                   ("E1", "n", square(par.W2), DH // 128, DM, "N1"),
                   ("E3", 0, relation(0, 0), 4, DM, None), ("E3", 1, relation(0, 1), 4, DM, None),
                   ("E3", "n", square(par.root1), 4, DM, "N3"),
                   ("N4", 0, relation(1, 0), 4, DM, "E3"), ("N4", 1, relation(1, 1), 4, DM, "E3"),
                   ("E4", "n", square(par.root2), 4, DM, "N4"),
                   ("N5", 0, square(par.W_qkv[:, 0:DM]), 4, DM, "E4"),
                   ("N5", 1, square(par.W_qkv[:, DM:2 * DM]), 4, DM, "E4"),
                   ("N5", 2, square(par.W_qkv[:, 2 * DM:]), 4, DM, None),
                   ("E5", "n", square(par.W_ff), 4, DM, "N5"),
                   ("N6", 0, square(par.W_l), 4, DM, "E5"), ("N6", 1, square(par.W_r), 4, DM, "E5")]

        def weights_before(p):
            return [(n, w) for n, w in enumerate(WEIGHTS) if w[0] == p]

        def need_weights(pe, count):
            pe.wait_ge(w_low, count)

        def load_weights(sp, p):
            for n, (_, _, source, k, width, _) in weights_before(p):
                if n:
                    sp.wait_ge(w_low, n)
                sp.dma_start(staged[:, 0:k * width].rearrange("p (k n) -> p k n", k=k), source).then_inc(w_loaded, 16)

        def split_weights_high(act, p):
            for n, (_, place, _, k, width, after) in weights_before(p):
                act.wait_ge(w_loaded, 16 * (n + 1))
                if after:
                    wait(act, product.through(after))
                src = staged[:, 0:k * width].rearrange("p (k n) -> p k n", k=k)
                nc.scalar.activation(halves(place)[0][:, 0:k, 0:width], src, ACT.Copy).then_inc(w_high, 1)

        def split_weights_low(dve, p):
            for n, (_, place, _, k, width, after) in weights_before(p):
                dve.wait_ge(w_high, n + 1)
                src = staged[:, 0:k * width].rearrange("p (k n) -> p k n", k=k)
                hi, lo = halves(place)
                nc.vector.tensor_tensor(lo[:, 0:k, 0:width], src, hi[:, 0:k, 0:width].bitcast(F32), ALU.subtract)\
                    .then_inc(w_low, 1)

        XIN_USED = {"N1": transposed, "E1": scaled, "N2": summed, "E2": scaled, "N3": summed, "E3": scaled,
                    "N4": transposed, "E4": scaled, "N5": transposed, "E5": transposed, "E6": scaled,
                    "N6": summed, "E7": transposed, "N7": transposed}
        PT_USED = {p: scanned if p in SCANNED else split for p in TRANSPOSED}
        AGG_USED = {"N2": summed, "N3": summed, "N4": evacuated, "N5": evacuated, "E5": transposed,
                    "N6": summed, "N7": silued}
        OUT_FILLED = {p: evacuated if p in ("N1", "E1", "E2", "E3", "E4", "E6", "E7") else
                      v_added if p == "E5" else finished for p in PASSES}
        STORES = {"N1": X.h, "E1": X.r1, "N2": X.g, "E2": X.r2, "N3": X.x1, "E3": X.r3, "N4": X.hb, "E4": X.r4,
                  "N5": X.x2, "E5": X.v, "E6": X.r5, "N6": X.x3, "E7": X.r6, "N7": out}
        LOADS = {"N1": x, "N2": X.h, "N3": X.g, "N4": X.x1, "N5": X.hb, "E6": X.v, "N6": X.x2, "N7": X.x3}
        STORE_LAG = {p: {"N5": 8, "N7": 9}.get(p, 7) for p in PASSES}
        WIDTH = {p: DH if p in ("N1", "E1", "N2", "E2") else DM for p in PASSES}
        IN_WIDTH = {p: DH if p in ("E1", "N2", "E2", "N3") else DM for p in PASSES}
        NAMES = list(PASSES)

        def before(p, passes):
            return ([q for q in NAMES[:NAMES.index(p)] if q in passes] or [None])[-1]

        block = ctx.enter_context(nc.Block())

        @block.sync
        def _(sp):
            for n, (a, source) in enumerate((
                    (b1, par.b1), (b2, par.b2), (bias1, par.bias1), (bias2, par.bias2), (bff, par.b_ff), (b3, par.b3))):
                sp.dma_start(a[:, :], source.partition_broadcast(128)).then_inc(consts_loaded, 16)
            sp.dma_start(bqkv[:, :, :].rearrange("p a n -> p (a n)"), par.b_qkv.partition_broadcast(128))\
                .then_inc(consts_loaded, 16)

            for p, n in PASSES.items():
                load_weights(sp, p)
                edge = p[0] == "E"
                if p in ("E3", "E4"):
                    if p == "E4":
                        wait(sp, gated.through("E3"))
                    sp.dma_start(gate[:, :, :].rearrange("p a n -> p (a n)"),
                                 par.gate[p == "E4"].rearrange("r d a -> (r d a)").partition_broadcast(128))\
                        .then_inc(consts_loaded, 16)
                if p in LOADS:
                    q = before(p, PASSES)
                    if q:
                        wait(sp, XIN_USED[q].through(q))
                    if p == "E6":
                        sp.wait_ge(softmax, 8)
                    if p != "N1":
                        maker = {"N2": "N1", "N3": "N2", "N4": "N3", "N5": "N4", "E6": "E5", "N6": "N5", "N7": "N6"}[p]
                        wait_all(sp, stored.through(maker))

                def load(step, p=p, edge=edge):
                    if step.c >= 4:
                        wait(sp, XIN_USED[p].free(p, step, 4))
                    at = (edge_rows if edge else node_rows)(LOADS[p], step)
                    s = loaded.slot(p, step)
                    sp.dma_start(xin[:, s, 0:IN_WIDTH[p]], at).then_inc(loaded.sem(p, step), 16)


                def load_residual(step, p=p):
                    s = res_in.slot(p, step)
                    if step.c >= 4:
                        wait(sp, y_ready.free(p, step, 4))
                    source = {"N3": x, "N5": X.x1, "N7": X.x3}[p]
                    sp.dma_start(res[:, s, :], node_rows(source, step)).then_inc(res_in.sem(p, step), 16)

                def store(step, p=p, edge=edge):
                    wait(sp, OUT_FILLED[p].done(p, step))
                    at = (edge_rows if edge else node_rows)(STORES[p], step)
                    sp.dma_start(at, outs[:, stored.slot(p, step), 0:WIDTH[p]]).then_inc(stored.sem(p, step), 16)

                if p in RESIDUAL:
                    q = before(p, RESIDUAL)
                    if q:
                        wait(sp, y_ready.through(q))
                    pipelined(sp, n, (0, load), (RESIDUAL[p], load_residual), (STORE_LAG[p], store))
                elif p in LOADS:
                    pipelined(sp, n, (0, load), (STORE_LAG[p], store))
                else:
                    pipelined(sp, n, (0, store))
            wait_all(sp, stored.through("N7"))

        @block.gpsimd
        def _(pool):
            pool.sem_inc(product.sem, 2)
            pool.sem_inc(evacuated.sem, 2)
            pool.sem_inc(finished.sem, 4)
            for s in range(4):
                pool.sem_inc(stored.sems[s], 16)

            nc.gpsimd.memset(half[:, :], -0.5).then_inc(half_set, 1)
            pool.wait_ge(half_set, 1)
            nc.gpsimd.memset(zero[:, :], 0.0).then_inc(zero_set, 1)

            def gather(p, step, ring, tile, width, table, source, column, copied):
                s = ring.slot(p, step)
                if p not in LISTED:
                    nc.gpsimd.tensor_copy(column[:, s:s + 1], col(table, step)).then_inc(copied.sem, 1)
                    wait(pool, copied.done(p, step))
                    settle(pool)
                pool.indirect_dma_start(
                    out=tile[:, s, 0:width], out_offset=None, in_=source,
                    in_offset=bass.IndirectOffsetOnAxis(ap=column[:, s:s + 1], axis=0),
                    bounds_check=source.shape[0] - 1, oob_is_err=False).then_inc(ring.sem(p, step), 16)

            for p, n in PASSES.items():
                src_pass = {"E1": "N1", "N2": "E1", "E2": "N2", "N3": "E2", "E3": "N3", "N4": "E3", "E4": "N4",
                            "N5": "E4", "E5": "N5", "N6": "E6", "E7": "N6", "N7": "E7"}.get(p)
                if not src_pass:
                    continue
                wait_all(pool, stored.through(src_pass))
                source = STORES[src_pass]
                edge = p[0] == "E"
                q = before(p, PASSES)
                if edge:
                    wait(pool, XIN_USED[q].through(q))
                qa = before(p, AGG_USED)
                if p in AGG_USED and qa:
                    wait(pool, AGG_USED[qa].through(qa))

                def gathers(step, p=p, source=source, edge=edge):
                    if p in LISTED:
                        wait(pool, listed.done(p, step))
                        settle(pool)
                        if p == "N2":
                            gather(p, step, agg_in, agg, DH, P.last_D, source, list_col[0], None)
                        else:
                            gather(p, step, agg_in, agg, DM, P.last_S0, source, list_col[0], None)
                        return
                    if edge:
                        if step.c >= 4:
                            wait(pool, XIN_USED[p].free(p, step, 4))
                            settle(pool)
                        side = P.S if p in ("E3", "E4") else P.D
                        gather(p, step, gathered, xin, IN_WIDTH[p], side.gather, source, list_col[0], list_copied)
                        if p == "E5":
                            gather(p, step, agg_in, agg, DM, P.receivers, source, list_col[1], list_copied2)
                        return
                    width = DH if p == "N3" else DM
                    if p in ("N3", "N7"):
                        if step.c >= 4:
                            wait(pool, AGG_USED[p].free(p, step, 4))
                            settle(pool)
                        nc.gpsimd.memset(agg[:, agg_in.slot(p, step), 0:width], 0.0).then_inc(prefilled.sem, 1)
                    wait(pool, (prefilled if p in ("N3", "N7") else bias_filled).done(p, step))
                    settle(pool)
                    gather(p, step, agg_in, agg, width, P.last_S0 if p == "N5" else P.last_D, source, list_col[0],
                           list_copied)
                    if p == "N5":
                        wait(pool, added.free(p, step, 4) if step.c >= 4 else added.through("N4"))
                        settle(pool)
                        nc.gpsimd.memset(agg2[:, agg2_in.slot(p, step), :], 0.0).then_inc(prefilled2.sem, 1)
                        wait(pool, prefilled2.done(p, step))
                        settle(pool)
                        gather(p, step, agg2_in, agg2, DM, P.last_S1, source, list_col[1], list_copied2)

                def gather_second(step, p=p, source=source):
                    wait(pool, listed2.done(p, step))
                    settle(pool)
                    gather(p, step, agg2_in, agg2, DM, P.last_S1, source, list_col[1], None)

                def inverse_norm(step, p=p):
                    s = step.c % 4
                    wait(pool, squared.done(p, step))
                    settle(pool)
                    nc.gpsimd.tensor_scalar(sq[:, s:s + 1], sq[:, s:s + 1], 1e-24, None, ALU.max).then_inc(bounded.sem, 1)
                    wait(pool, bounded.done(p, step))
                    nc.gpsimd.tensor_tensor(rn[:, s:s + 1], sq[:, s:s + 1], half[:, 0:1], ALU.pow).then_inc(inv_norm.sem, 1)

                def inverse_std(step, p=p):
                    s = step.c % 4
                    wait(pool, var_ready.done(p, step))
                    nc.gpsimd.tensor_tensor(rstd[:, s:s + 1], ve[:, s:s + 1], half[:, 0:1], ALU.pow).then_inc(rstd_ready.sem, 1)

                stages = [(0, gathers)]
                if p == "N4":
                    stages += [(1, gather_second)]
                if p == "N3":
                    stages += [(4, inverse_norm)]
                if p in NORMED:
                    stages += [({"N3": 6, "N5": 5, "N6": 4, "N7": 6}[p], inverse_std)]
                pipelined(pool, n, *stages)

        @block.tensor
        def _(pe):

            def transpose(p, step, tile, width, bank=None, tell=True):
                s = step.c % 2 if bank is None else bank
                for k in range(width // 128):
                    last = nc.tensor.transpose(pT[:, s, k * 128:(k + 1) * 128], tile[:, k * 128:(k + 1) * 128], P.ident[:, :])
                if tell:
                    last.then_inc(transposed.sem, 1)

            def multiply(dst, hi, lo, w_hi, w_lo, k_tiles, width):
                for k in range(k_tiles):
                    at = slice(k * 128, (k + 1) * 128)
                    nc.tensor.matmul(dst[:, 0:width], hi[:, at], w_hi(k), start=k == 0, stop=False)
                    nc.tensor.matmul(dst[:, 0:width], hi[:, at], w_lo(k), start=False, stop=False)
                    last = nc.tensor.matmul(dst[:, 0:width], lo[:, at], w_hi(k), start=False, stop=k == k_tiles - 1)
                return last

            for p, n in PASSES.items():
                if p not in TRANSPOSED:
                    continue
                q = before(p, TRANSPOSED)
                if q:
                    wait(pe, PT_USED[q].through(q))
                    wait(pe, evacuated.through(q))
                if p in ("E3", "E4"):
                    type0 = pe.value_load(P.type0_tiles[0:1, 0:1], min_val=0, max_val=S_TILES)
                need_weights(pe, sum(NAMES.index(w[0]) <= NAMES.index(p) for w in WEIGHTS))

                def turn(step, p=p):
                    s4, s2 = step.c % 4, step.c % 2
                    if p in ("N1", "N4", "N5", "N7", "E7"):
                        wait(pe, xin_in(p).done(p, step))
                        tile = xin[:, xin_in(p).slot(p, step), :]
                    elif p == "N3":
                        wait(pe, summed.done(p, step))
                        tile = scan[:, s2, :]
                    else:
                        wait(pe, scaled.done(p, step))
                        tile = y[:, s4, :]
                    if step.c >= 2:
                        wait(pe, PT_USED[p].free(p, step, 2))
                    transpose(p, step, tile, DH if p in ("E1", "E2", "N3") else DM)

                def turn_back(step, p=p):
                    s2 = step.c % 2
                    wait(pe, scanned.done(p, step))
                    wait(pe, evacuated.free(p, step, 2))
                    for k in range(DH // 128):
                        last = nc.tensor.transpose(pM[:, s2, k * 128:(k + 1) * 128], scan[:, s2, k * 128:(k + 1) * 128],
                                                   P.ident[:, :])
                    last.then_inc(product.sem, 1)

                def dense(step, p=p):
                    s2 = step.c % 2
                    wait(pe, split.done(p, step))
                    wait(pe, evacuated.free(p, step, 2))
                    if p in ("E3", "E4"):
                        kind = step.t >= type0

                        def w(half_):
                            return lambda k: half_[:, bass.ds(kind, 1), k, :].rearrange("p a n -> p (a n)")
                        w_hi, w_lo = w(we_hi), w(we_lo)
                    elif p in ("E7", "N7"):
                        place = 0 if p == "E7" else 1
                        w_hi, w_lo = (lambda k: we_hi[:, place, k, :]), (lambda k: we_lo[:, place, k, :])
                    else:
                        width = DH if p == "N1" else DM
                        w_hi, w_lo = (lambda k: wn_hi[:, k, 0:width]), (lambda k: wn_lo[:, k, 0:width])
                    multiply(pM[:, s2, :], xT_hi[:, s2, :], xT_lo[:, s2, :], w_hi, w_lo,
                             2 if p == "N3" else 4, DH if p == "N1" else DM).then_inc(product.sem, 1)

                def turn_pair(step, p=p):
                    wait(pe, xin_in(p).done(p, step))
                    wait(pe, agg_in.done(p, step))
                    if step.c >= 1:
                        wait(pe, split.free(p, step, 1))
                    transpose(p, step, xin[:, xin_in(p).slot(p, step), :], DM, 0, False)
                    transpose(p, step, agg[:, agg_in.slot(p, step), :], DM, 1)

                def qkv(step, p=p):
                    s2 = step.c % 2
                    wait(pe, split.done(p, step))
                    if step.c >= 1:
                        wait(pe, v_added.free(p, step, 1))
                    multiply(pM[:, 4, :], xT_hi[:, s2, :], xT_lo[:, s2, :], lambda k: we_hi[:, 2, k, :],
                             lambda k: we_lo[:, 2, k, :], 4, DM).then_inc(v_done.sem, 1)
                    if step.c >= 2:
                        wait(pe, qk_added.free(p, step, 2))
                    multiply(pM[:, s2, :], xT_hi[:, s2, :], xT_lo[:, s2, :], lambda k: we_hi[:, 1, k, :],
                             lambda k: we_lo[:, 1, k, :], 4, DM)
                    multiply(pM[:, 2 + s2, :], rT_hi[:, s2, :], rT_lo[:, s2, :], lambda k: we_hi[:, 0, k, :],
                             lambda k: we_lo[:, 0, k, :], 4, DM).then_inc(product.sem, 1)

                def turn_scores(step, p=p):
                    wait(pe, scored.done(p, step))
                    if step.c >= 1:
                        wait(pe, score_kept.free(p, step, 1))
                    nc.tensor.transpose(pM[0:HEADS, 5, 0:128], scores[:, step.c % 2, :], P.ident[:, :])\
                        .then_inc(score_T.sem, 1)

                def turn_att(step, p=p):
                    s2 = step.c % 2
                    wait(pe, att_cut.done(p, step))
                    if step.c >= 2:
                        wait(pe, scaled.free(p, step, 2))
                    settle(pe)
                    nc.tensor.transpose(pM[:, 4 + s2, 0:HEADS], att[:, s2, :], P.ident[0:HEADS, 0:HEADS])\
                        .then_inc(att_T.sem, 1)

                if p in ("E1", "E2"):
                    pipelined(pe, n, (0, turn), (1, turn_back))
                elif p == "E5":
                    pipelined(pe, n, (0, turn_pair), (1, qkv), (2, turn_scores))
                elif p == "E6":
                    pipelined(pe, n, (0, turn_att), (1, turn), (3, dense))
                elif p in ("E3", "E4", "E7"):
                    pipelined(pe, n, (0, turn), (2, dense))
                else:
                    pipelined(pe, n, (0, turn), (1, dense))

        @block.scalar
        def _(act):
            act.wait_ge(consts_loaded, 7 * 16)
            act.wait_ge(zero_set, 1)
            for p, n in PASSES.items():
                split_weights_high(act, p)
                if p in DENSE and p != "N1":
                    wait(act, product.through(before(p, TRANSPOSED)))

                def take_high(step, p=p):
                    s2 = step.c % 2
                    wait(act, scanned.done(p, step) if p in SCANNED else transposed.done(p, step))
                    wait(act, product.free(p, step, 2))
                    width = DH if p == "N3" else DM
                    source = scan[:, s2, 0:width] if p in SCANNED else pT[:, s2, 0:width]
                    nc.scalar.activation(xT_hi[:, s2, 0:width], source, ACT.Copy).then_inc(high.sem, 1)

                def take_high_pair(step, p=p):
                    s2 = step.c % 2
                    wait(act, transposed.done(p, step))
                    wait(act, product.free(p, step, 2))
                    nc.scalar.activation(xT_hi[:, s2, :], pT[:, 0, :], ACT.Copy)
                    nc.scalar.activation(rT_hi[:, s2, :], pT[:, 1, :], ACT.Copy).then_inc(high.sem, 1)

                def h_out(step, p=p):
                    wait(act, product.done(p, step))
                    wait(act, stored.free(p, step))
                    settle(act)
                    nc.scalar.activation(outs[:, stored.slot(p, step), 0:DH], pM[:, step.c % 2, 0:DH], ACT.Copy,
                                         scale=col(P.dinv, step)).then_inc(evacuated.sem, 1)

                def scale_edge(step, p=p):
                    s = step.c % 4
                    wait(act, xin_in(p).done(p, step))
                    if step.c >= 4:
                        wait(act, transposed.free(p, step, 4))
                    width = IN_WIDTH[p]
                    if p in ("E3", "E4"):
                        wait(act, gated.done(p, step))
                        nc.scalar.activation(g[:, s:s + 1], z[:, s:s + 1], ACT.Sigmoid).then_inc(sigmoid.sem, 1)
                        wait(act, sigmoid.done(p, step))
                        scale = g[:, s:s + 1]
                    else:
                        settle(act)
                        scale = col(P.weights, step)
                    nc.scalar.activation(y[:, s, 0:width], xin[:, xin_in(p).slot(p, step), 0:width], ACT.Copy, scale=scale)\
                        .then_inc(scaled.sem, 1)

                def copy_out(step, p=p):
                    wait(act, product.done(p, step))
                    wait(act, stored.free(p, step))
                    nc.scalar.activation(outs[:, stored.slot(p, step), 0:WIDTH[p]], pM[:, step.c % 2, 0:WIDTH[p]], ACT.Copy)\
                        .then_inc(evacuated.sem, 1)

                def prefill(step, p=p):
                    if step.c >= 4:
                        wait(act, AGG_USED[p].free(p, step, 4))
                    bias = bias2 if p == "N5" else bff
                    nc.scalar.activation(agg[:, agg_in.slot(p, step), :], bias[:, :], ACT.Copy).then_inc(bias_filled.sem, 1)

                def list_nodes(step, p=p):
                    s = agg_in.slot(p, step)
                    if step.c >= 4:
                        wait(act, agg_in.done(p, step.back(4)))
                        wait(act, AGG_USED[p].free(p, step, 4))
                    if p == "N2":
                        nc.scalar.activation(agg[:, s, 0:DH], zero[:, 0:1].broadcast_to([128, DH]), ACT.Copy)
                    else:
                        nc.scalar.activation(agg[:, s, :], bias1[:, :], ACT.Copy)
                    nc.scalar.activation(list_col[0][:, s:s + 1], col(P.last_D if p == "N2" else P.last_S0, step), ACT.Copy)\
                        .then_inc(listed.sem, 1)

                def list_second(step, p=p):
                    s = agg2_in.slot(p, step)
                    if step.c >= 4:
                        wait(act, agg2_in.done(p, step.back(4)))
                        wait(act, added.free(p, step, 4))
                    nc.scalar.activation(agg2[:, s, :], zero[:, 0:1].broadcast_to([128, DM]), ACT.Copy)
                    nc.scalar.activation(list_col[1][:, s:s + 1], col(P.last_S1, step), ACT.Copy).then_inc(listed2.sem, 1)

                def relu_out(step, p=p):
                    wait(act, added.done(p, step))
                    wait(act, stored.free(p, step))
                    nc.scalar.activation(outs[:, stored.slot(p, step), :], y[:, step.c % 4, :], ACT.Relu)\
                        .then_inc(finished.sem, 1)

                def sum_squares(step, p=p):
                    s = step.c % 4
                    wait(act, evacuated.done(p, step))
                    if step.c >= 1:
                        wait(act, squared.free(p, step, 1))
                    nc.scalar.activation(prod[:, :], y[:, s, :], ACT.Square, accum_out=sq[:, s:s + 1])\
                        .then_inc(squared.sem, 1)

                def silu(step, p=p):
                    wait(act, biased.done(p, step))
                    if step.c >= 2:
                        wait(act, y_ready.free(p, step, 2))
                    nc.scalar.activation(scan[:, step.c % 2, :], agg[:, agg_in.slot(p, step), :], ACT.Silu).then_inc(silued.sem, 1)

                def norm_out(step, p=p):
                    s = step.c % 4
                    wait(act, shift_ready.done(p, step))
                    wait(act, stored.free(p, step))
                    nc.scalar.activation(outs[:, stored.slot(p, step), :], y[:, s, :], ACT.Identity,
                                         scale=rstd[:, s:s + 1], bias=nb[:, s:s + 1]).then_inc(finished.sem, 1)

                def keep_scores(step, p=p):
                    wait(act, score_T.done(p, step))
                    settle(act)
                    nc.scalar.activation(srow[:, bass.ds(step.number(0, 128), 128)], pM[0:HEADS, 5, 0:128], ACT.Copy,
                                         scale=float(DK) ** -0.5).then_inc(score_kept.sem, 1)

                def cut_att(step, p=p):
                    if step.c >= 2:
                        wait(act, att_T.free(p, step, 2))
                        settle(act)
                    nc.scalar.activation(att[:, step.c % 2, :], srow[:, bass.ds(step.number(0, 128), 128)], ACT.Copy)\
                        .then_inc(att_cut.sem, 1)

                if p in ("N2", "N4", "N5", "N6") and before(p, AGG_USED):
                    qa = before(p, AGG_USED)
                    wait(act, AGG_USED[qa].through(qa))
                    wait_all(act, agg_in.through(qa))
                if p in LISTED:
                    wait_all(act, gathered.through(p))
                if p == "N1":
                    pipelined(act, n, (0, take_high), (2, h_out))
                elif p in ("E1", "E2"):
                    pipelined(act, n, (0, scale_edge), (2, copy_out))
                elif p == "N2":
                    pipelined(act, n, (0, list_nodes))
                elif p == "N3":
                    pipelined(act, n, (6, norm_out), (0, take_high), (2, sum_squares))
                elif p in ("E3", "E4"):
                    pipelined(act, n, (0, scale_edge), (1, take_high))
                elif p == "N4":
                    pipelined(act, n, (0, list_nodes), (1, list_second), (2, take_high), (5, relu_out))
                elif p == "N5":
                    pipelined(act, n, (0, prefill), (2, take_high), (7, norm_out))
                elif p == "E5":
                    pipelined(act, n, (0, take_high_pair), (2, keep_scores))
                    act.wait_ge(softmax, 4)
                    nc.scalar.activation(srow[:, :], srow[:, :], ACT.Exp).then_inc(exps, 1)
                    act.wait_ge(softmax, 8)
                elif p == "E6":
                    pipelined(act, n, (0, cut_att), (2, take_high))
                elif p == "N6":
                    pipelined(act, n, (6, norm_out), (0, prefill))
                elif p == "E7":
                    pipelined(act, n, (0, take_high), (3, copy_out))
                elif p == "N7":
                    pipelined(act, n, (0, take_high), (3, silu), (7, norm_out))

        @block.vector
        def _(dve):
            dve.wait_ge(consts_loaded, 7 * 16)
            for p, n in PASSES.items():
                split_weights_low(dve, p)
                dp = DM if p not in ("E1", "E2") else DH
                if p in ("E3", "E4"):
                    type0 = dve.value_load(P.type0_tiles[0:1, 0:1], min_val=0, max_val=S_TILES)
                    dve.wait_ge(consts_loaded, (8 if p == "E3" else 9) * 16)

                def take_low(step, p=p):
                    s2 = step.c % 2
                    wait(dve, high.done(p, step))
                    width = DH if p == "N3" else DM
                    source = scan[:, s2, 0:width] if p in SCANNED else pT[:, s2, 0:width]
                    nc.vector.tensor_tensor(xT_lo[:, s2, 0:width], source, xT_hi[:, s2, 0:width].bitcast(F32),
                                            ALU.subtract).then_inc(split.sem, 1)

                def take_low_pair(step, p=p):
                    s2 = step.c % 2
                    wait(dve, high.done(p, step))
                    nc.vector.tensor_tensor(xT_lo[:, s2, :], pT[:, 0, :], xT_hi[:, s2, :].bitcast(F32), ALU.subtract)
                    nc.vector.tensor_tensor(rT_lo[:, s2, :], pT[:, 1, :], rT_hi[:, s2, :].bitcast(F32), ALU.subtract)\
                        .then_inc(split.sem, 1)

                def run_sums(step, p=p, dp=dp):
                    s2 = step.c % 2
                    side = P.S if p in ("E3", "E4") else P.D
                    wait(dve, transposed.done(p, step))
                    if step.c >= 1:
                        wait(dve, scanned.free(p, step, 1))
                    if step.c >= 2:
                        wait(dve, product.free(p, step, 2) if p in ("E1", "E2") else split.free(p, step, 2))
                    for k in range(dp // 128):
                        last = nc.vector.tensor_tensor_scan(
                            scan[:, s2, k * 128:(k + 1) * 128], side.same_run[:, bass.ds(step.number(0, 128), 128)],
                            pT[:, s2, k * 128:(k + 1) * 128],
                            0.0 if step.c == 0 and step.i is None else scan[:, 1 - s2, k * 128 + 127:k * 128 + 128],
                            ALU.mult, ALU.add)
                    last.then_inc(scanned.sem, 1)

                def sum_rows(step, p=p):
                    s = step.c % 4
                    wait(dve, xin_in(p).done(p, step))
                    wait(dve, agg_in.done(p, step))
                    width = DM if p == "N6" else DH
                    if p == "N3":
                        if step.c >= 2:
                            wait(dve, transposed.free(p, step, 2))
                        into = scan[:, step.c % 2, 0:width]
                    else:
                        wait(dve, finished.free(p, step, 4))
                        into = y[:, s, 0:width]
                    nc.vector.tensor_tensor(into, xin[:, xin_in(p).slot(p, step), 0:width],
                                            agg[:, agg_in.slot(p, step), 0:width], ALU.add).then_inc(summed.sem, 1)

                def scale_rows(step, p=p):
                    s = step.c % 4
                    wait(dve, summed.done(p, step))
                    nc.vector.scalar_tensor_tensor(y[:, s, 0:DH], y[:, s, 0:DH], col(P.dinv, step), b1[:, :],
                                                   ALU.mult, ALU.add).then_inc(added.sem, 1)

                def relu_scaled(step, p=p):
                    wait(dve, added.done(p, step))
                    wait(dve, stored.free(p, step))
                    nc.vector.tensor_scalar(outs[:, stored.slot(p, step), 0:DH], y[:, step.c % 4, 0:DH], 0.0,
                                            col(P.dinv, step), ALU.max, ALU.mult).then_inc(finished.sem, 1)

                def gcn_out(step, p=p):
                    wait(dve, product.done(p, step))
                    wait(dve, finished.free(p, step, 4))
                    nc.vector.scalar_tensor_tensor(y[:, step.c % 4, :], pM[:, step.c % 2, :], col(P.dinv, step), b2[:, :],
                                                   ALU.mult, ALU.add).then_inc(evacuated.sem, 1)

                def normalise(step, p=p):
                    s = step.c % 4
                    wait(dve, inv_norm.done(p, step))
                    wait(dve, res_in.done(p, step))
                    nc.vector.scalar_tensor_tensor(y[:, s, :], y[:, s, :], rn[:, s:s + 1], res[:, res_in.slot(p, step), :],
                                                   ALU.mult, ALU.add).then_inc(y_ready.sem, 1)

                def statistics(step, p=p):
                    s = step.c % 4
                    wait(dve, (summed if p == "N6" else y_ready).done(p, step))
                    nc.vector.bn_stats(stats[:, s, :], y[:, s, :]).then_inc(bn_done.sem, 1)

                def variance(step, p=p):
                    s = step.c % 4
                    wait(dve, bn_done.done(p, step))
                    settle(dve)
                    nc.vector.bn_aggr(mv[:, s, :], stats[:, s, :]).then_inc(mean_ready.sem, 1)
                    wait(dve, mean_ready.done(p, step))
                    nc.vector.tensor_scalar(ve[:, s:s + 1], mv[:, s, 1:2], 1e-5, None, ALU.add).then_inc(var_ready.sem, 1)

                def shift(step, p=p):
                    s = step.c % 4
                    wait(dve, rstd_ready.done(p, step))
                    nc.vector.scalar_tensor_tensor(nb[:, s:s + 1], mv[:, s, 0:1], -1.0, rstd[:, s:s + 1],
                                                   ALU.mult, ALU.mult).then_inc(shift_ready.sem, 1)

                def dot_gate(step, p=p):
                    s = step.c % 4
                    wait(dve, xin_in(p).done(p, step))
                    if step.c >= 1:
                        wait(dve, gated.free(p, step, 1))
                    if step.c >= 4:
                        wait(dve, sigmoid.free(p, step, 4))
                    kind = step.t >= type0
                    nc.vector.scalar_tensor_tensor(
                        prod[:, :], xin[:, xin_in(p).slot(p, step), :], 1.0,
                        gate[:, bass.ds(kind, 1), :].rearrange("p a n -> p (a n)"),
                        ALU.mult, ALU.mult, accum_out=z[:, s:s + 1]).then_inc(gated.sem, 1)

                def message_out(step, p=p):
                    wait(dve, product.done(p, step))
                    wait(dve, stored.free(p, step))
                    bias = {"E3": bias1, "E4": bias2, "E6": bff}[p]
                    scale = 1.0 if p == "E6" else col(P.is_type0, step)
                    nc.vector.scalar_tensor_tensor(outs[:, stored.slot(p, step), :], bias[:, :], scale, pM[:, step.c % 2, :],
                                                   ALU.mult, ALU.add).then_inc(evacuated.sem, 1)

                def add_first(step, p=p):
                    wait(dve, product.done(p, step))
                    wait(dve, agg_in.done(p, step))
                    wait(dve, finished.free(p, step, 4))
                    nc.vector.tensor_tensor(y[:, step.c % 4, :], pM[:, step.c % 2, :], agg[:, agg_in.slot(p, step), :],
                                            ALU.add).then_inc(evacuated.sem, 1)

                def add_second(step, p=p):
                    s = step.c % 4
                    wait(dve, evacuated.done(p, step))
                    wait(dve, agg2_in.done(p, step))
                    nc.vector.tensor_tensor(y[:, s, :], y[:, s, :], agg2[:, agg2_in.slot(p, step), :], ALU.add)\
                        .then_inc(added.sem, 1)

                def add_residual(step, p=p):
                    s = step.c % 4
                    wait(dve, added.done(p, step))
                    wait(dve, res_in.done(p, step))
                    nc.vector.tensor_tensor(y[:, s, :], y[:, s, :], res[:, res_in.slot(p, step), :], ALU.add)\
                        .then_inc(y_ready.sem, 1)

                def add_values(step, p=p):
                    wait(dve, v_done.done(p, step))
                    wait(dve, stored.free(p, step))
                    nc.vector.tensor_tensor(outs[:, stored.slot(p, step), :], pM[:, 4, :], bqkv[:, 2, :], ALU.add)\
                        .then_inc(v_added.sem, 1)

                def add_qk(step, p=p):
                    s = step.c % 4
                    s2 = step.c % 2
                    wait(dve, product.done(p, step))
                    if step.c >= 1:
                        wait(dve, scored.free(p, step, 1))
                    nc.vector.tensor_tensor(y[:, s, :], pM[:, s2, :], bqkv[:, 1, :], ALU.add)
                    nc.vector.tensor_tensor(prod[:, :], pM[:, 2 + s2, :], bqkv[:, 0, :], ALU.add).then_inc(qk_added.sem, 1)

                def multiply_qk(step, p=p):
                    s = step.c % 4
                    wait(dve, qk_added.done(p, step))
                    nc.vector.tensor_tensor(y[:, s, :], y[:, s, :], prod[:, :], ALU.mult).then_inc(multiplied.sem, 1)

                def score(step, p=p):
                    wait(dve, multiplied.done(p, step))
                    if step.c >= 2:
                        wait(dve, score_T.free(p, step, 2))
                    nc.vector.reduce_sum(scores[:, step.c % 2, :], y[:, step.c % 4, :].rearrange("p (h d) -> p h d", h=HEADS),
                                         AX.X).then_inc(scored.sem, 1)

                def weigh_values(step, p=p):
                    s = step.c % 4
                    wait(dve, xin_in(p).done(p, step))
                    wait(dve, att_T.done(p, step))
                    if step.c >= 4:
                        wait(dve, transposed.free(p, step, 4))
                    nc.vector.tensor_tensor(
                        y[:, s, :].rearrange("p (h d) -> p h d", h=HEADS),
                        xin[:, xin_in(p).slot(p, step), :].rearrange("p (h d) -> p h d", h=HEADS),
                        pM[:, 4 + step.c % 2, 0:HEADS].unsqueeze(2).broadcast_to([128, HEADS, DK]), ALU.mult)\
                        .then_inc(scaled.sem, 1)

                def sage_sum(step, p=p):
                    wait(dve, product.done(p, step))
                    wait(dve, agg_in.done(p, step))
                    tile = agg[:, agg_in.slot(p, step), :]
                    nc.vector.scalar_tensor_tensor(tile, tile, col(P.rdeg, step), pM[:, step.c % 2, :],
                                                   ALU.mult, ALU.add).then_inc(evacuated.sem, 1)

                def sage_bias(step, p=p):
                    tile = agg[:, agg_in.slot(p, step), :]
                    wait(dve, evacuated.done(p, step))
                    nc.vector.tensor_tensor(tile, tile, b3[:, :], ALU.add).then_inc(biased.sem, 1)

                def sage_residual(step, p=p):
                    s = step.c % 4
                    wait(dve, silued.done(p, step))
                    wait(dve, res_in.done(p, step))
                    wait(dve, finished.free(p, step, 4))
                    nc.vector.tensor_tensor(y[:, s, :], scan[:, step.c % 2, :], res[:, res_in.slot(p, step), :], ALU.add)\
                        .then_inc(y_ready.sem, 1)

                def soft_max(dve):
                    E = D_TILES * 128
                    flat = rows[0:HEADS, :, :, :].rearrange("p a b n -> p (a b n)")
                    run = flat[:, 0:E]
                    cut = flat[:, E:E + E // 2 + 2].bitcast(BF16)[:, 0:E + 1]
                    same = P.D.same_run[0:HEADS, :]
                    wait(dve, score_kept.through("E5"))
                    nc.vector.tensor_scalar(cut, same[:, :], -1.0, 1e30, ALU.add, ALU.mult).then_inc(softmax, 1)
                    dve.wait_ge(softmax, 1)
                    nc.vector.tensor_tensor_scan(run, cut[:, 0:E], srow[:, :], -1e30, ALU.add, ALU.max).then_inc(softmax, 1)
                    dve.wait_ge(softmax, 2)
                    nc.vector.tensor_tensor_scan(run[:, ::-1], cut[:, E:0:-1], run[:, ::-1], -1e30, ALU.add, ALU.max)\
                        .then_inc(softmax, 1)
                    dve.wait_ge(softmax, 3)
                    nc.vector.tensor_tensor(srow[:, :], srow[:, :], run, ALU.subtract).then_inc(softmax, 1)
                    dve.wait_ge(exps, 1)
                    nc.vector.tensor_tensor_scan(run, same[:, 0:E], srow[:, :], 0.0, ALU.mult, ALU.add).then_inc(softmax, 1)
                    dve.wait_ge(softmax, 5)
                    nc.vector.tensor_tensor_scan(run[:, ::-1], same[:, E:0:-1], run[:, ::-1], 0.0, ALU.mult, ALU.max)\
                        .then_inc(softmax, 1)
                    dve.wait_ge(softmax, 6)
                    nc.vector.reciprocal(run, run).then_inc(softmax, 1)
                    dve.wait_ge(softmax, 7)
                    nc.vector.tensor_tensor(srow[:, :], srow[:, :], run, ALU.mult).then_inc(softmax, 1)

                if p == "N1":
                    pipelined(dve, n, (0, take_low))
                elif p in ("E1", "E2"):
                    pipelined(dve, n, (0, run_sums))
                elif p == "N2":
                    pipelined(dve, n, (0, sum_rows), (1, scale_rows), (2, relu_scaled))
                elif p == "N3":
                    pipelined(dve, n, (4, statistics), (0, sum_rows), (4, variance), (1, take_low), (2, gcn_out), (3, normalise),
                              (5, shift))
                elif p in ("E3", "E4"):
                    pipelined(dve, n, (0, dot_gate), (1, run_sums), (2, take_low), (3, message_out))
                elif p == "N4":
                    pipelined(dve, n, (0, take_low), (1, add_first), (2, add_second))
                elif p == "N5":
                    pipelined(dve, n, (3, statistics), (0, take_low), (3, variance), (2, add_second), (4, shift),
                              (1, add_first), (2, add_residual))
                elif p == "E5":
                    pipelined(dve, n, (0, take_low_pair), (1, add_values), (1, add_qk), (1, multiply_qk), (1, score))
                    soft_max(dve)
                elif p == "E6":
                    pipelined(dve, n, (0, weigh_values), (1, run_sums), (2, take_low), (3, message_out))
                elif p == "N6":
                    pipelined(dve, n, (1, statistics), (3, shift), (1, variance), (0, sum_rows))
                elif p == "E7":
                    pipelined(dve, n, (0, run_sums), (1, take_low))
                elif p == "N7":
                    pipelined(dve, n, (5, statistics), (0, take_low), (5, variance), (1, sage_sum), (6, shift),
                              (4, sage_residual), (2, sage_bias))


def gnn_kernel(nc, x, src, dst, edge_type, edge_weight, par, out):
    ctx = ExitStack()
    with ctx:
        def sb(name, shape, dt=F32):
            return ctx.enter_context(nc.sbuf_tensor(name, shape, dt))

        def dram(name, rows, width):
            return nc.dram_tensor("rows_" + name, [rows, width], F32).ap()

        P = Named()
        P.ident = sb("ident", [128, 128])
        P.D = Ordering(D_TILES, NODE_COLS, sb("gather_D", [128, D_TILES], I32),
                       sb("same_run_D", [128, D_TILES * 128 + 1], BF16))
        P.S = Ordering(S_TILES, 2 * NODE_COLS, sb("gather_S", [128, S_TILES], I32),
                       sb("same_run_S", [128, S_TILES * 128 + 1], BF16))
        P.receivers, P.weights = sb("receivers", [128, D_TILES], I32), sb("weights", [128, D_TILES])
        P.type0_tiles, P.is_type0 = sb("type0_tiles", [128, 1], I32), sb("is_type0", [128, S_TILES])
        P.last_D, P.last_S0, P.last_S1 = (sb(n, [128, NODE_STEPS], I32) for n in ("last_D", "last_S0", "last_S1"))
        P.dinv, P.rdeg = sb("dinv", [128, NODE_STEPS]), sb("rdeg", [128, NODE_STEPS])

        X = Named()
        X.h, X.g = dram("h", N, DH), dram("g", N, DH)
        X.x1, X.hb, X.x2, X.x3 = (dram(name, N, DM) for name in ("x1", "hb", "x2", "x3"))
        X.r1, X.r2 = (dram(name, D_TILES * 128, DH) for name in ("r1", "r2"))
        X.r3, X.r4 = (dram(name, S_TILES * 128, DM) for name in ("r3", "r4"))
        X.v, X.r5, X.r6 = (dram(name, D_TILES * 128, DM) for name in ("v", "r5", "r6"))
        X.mixed = [dram(f"mixed{l}", 8, 128 * DM) for l in range(2)]
        prepare(nc, P, src, dst, edge_type, edge_weight)
        combine_bases(nc, X.mixed, par.att, par.basis)
        layers_block(nc, P, x, out, par, X)


_INS = ['x', 'src', 'dst', 'edge_type_2', 'edge_weight', 'L0_gnn_W1', 'L0_gnn_b1', 'L0_gnn_W2', 'L0_gnn_b2',
        'L1_gnn_basis1', 'L1_gnn_att1', 'L1_gnn_gate_w1', 'L1_gnn_root1', 'L1_gnn_bias1',
        'L1_gnn_basis2', 'L1_gnn_att2', 'L1_gnn_gate_w2', 'L1_gnn_root2', 'L1_gnn_bias2',
        'L2_gnn_W_qkv', 'L2_gnn_b_qkv', 'L2_gnn_W_ff', 'L2_gnn_b_ff', 'L3_gnn_W_l', 'L3_gnn_W_r', 'L3_gnn_b']
_TRANSPOSED = ('L2_gnn_W_qkv', 'L2_gnn_W_ff')


def kernel(**inputs):
    import numpy as _np
    import concourse.bacc as _bacc
    from concourse import mybir as _mybir
    from concourse.bass_utils import run_bass_kernel_spmd as _run

    nc = _bacc.Bacc("TRN2", target_bir_lowering=False, num_devices=1)
    arrays, aps = {}, {}
    for name in _INS:
        a = _np.asarray(inputs[name])
        a = _np.ascontiguousarray(a.T if name in _TRANSPOSED else a)
        arrays[f"in_{name}_dram"] = a
        aps[name] = nc.dram_tensor(f"in_{name}_dram", a.shape, _mybir.dt.from_np(a.dtype), kind="ExternalInput").ap()
    out = nc.dram_tensor("out_0_dram", (N, DM), F32, kind="ExternalOutput").ap()
    par = Named()
    par.W1, par.b1, par.W2, par.b2 = (aps[f"L0_gnn_{n}"] for n in ("W1", "b1", "W2", "b2"))
    par.basis, par.att, par.gate = ([aps[f"L1_gnn_{n}{l}"] for l in (1, 2)] for n in ("basis", "att", "gate_w"))
    par.root1, par.root2, par.bias1, par.bias2 = (aps[f"L1_gnn_{n}"] for n in ("root1", "root2", "bias1", "bias2"))
    par.W_qkv, par.b_qkv, par.W_ff, par.b_ff = (aps[f"L2_gnn_{n}"] for n in ("W_qkv", "b_qkv", "W_ff", "b_ff"))
    par.W_l, par.W_r, par.b3 = (aps[f"L3_gnn_{n}"] for n in ("W_l", "W_r", "b"))
    gnn_kernel(nc, aps["x"], aps["src"], aps["dst"], aps["edge_type_2"], aps["edge_weight"], par, out)
    r = _run(nc, [arrays], core_ids=[0])
    return r.results[0]["out_0_dram"]
```

```python
import concourse.bass as bass
from concourse import mybir
from contextlib import ExitStack

F32, F32R, BF16, I32 = mybir.dt.float32, mybir.dt.float32r, mybir.dt.bfloat16, mybir.dt.int32
ALU, ACT, AX = mybir.AluOpType, mybir.ActivationFunctionType, mybir.AxisListType

N, EDGES, DM, DH = 10000, 5000, 512, 256
HEADS, DK = 8, 64
RELATIONS, BASES = 2, 30
NODE_COLS = -(-N // 128)
NODE_SPAN = NODE_COLS * 128
NODE_STEPS = NODE_COLS
ET, EP = 40, 125
D_TILES = -(-EDGES // 128)
S_TILES = D_TILES + 1
NO_ROW = 1 << 20
MIX_D, MIX_PLACE = 6, 12
WIDE = S_TILES * 128 + 128


def over_columns(pe, product):
    for t in range(8):
        product(t, t == 0, False)
    with pe.Fori(1, ET // 8 - 1) as i:
        for m in range(8):
            product(8 * i + m, False, False)
    for t in range(ET - 8, ET):
        last = product(t, False, t == ET - 1)
    return last


def prepare(nc, persist, src, dst, edge_type, edge_weight, mixed_w, att, basis):
    P = persist
    tag = {"D": P.D, "S": P.S}
    pos_dram = {n: nc.dram_tensor(f"prep_node_{n}", [NODE_COLS * 128], F32).ap() for n in range(5)}
    seg_dram = {d: nc.dram_tensor(f"prep_ids_{d}", [tag[d].tiles * 128 + 1], F32).ap() for d in "DS"}

    ctx = ExitStack()
    with ctx:
        def sb(name, shape, dt=F32):
            return ctx.enter_context(nc.sbuf_tensor(name, shape, dt))

        def sem(name):
            return ctx.enter_context(nc.semaphore(name))

        raw_i = sb("raw_i", [ET, 3, EP], I32)
        raw_f = sb("raw_f", [ET, 4, EP])
        edge = sb("edge", [EP, 4, ET])
        edge_i = sb("edge_i", [EP, 2, ET], I32)
        part_i = sb("part_i", [EP, 2, ET], I32)
        lo = sb("lo", [EP, 2, ET])
        hi = sb("hi", [EP, 2, ET])
        key_bc = {d: sb(f"key_bc_{d}", [128, WIDE], I32) for d in "DS"}
        low_bc = sb("low_bc", [128, WIDE], I32)
        iota_i = sb("iota_i", [128, 2 * NODE_COLS], I32)
        iota = sb("iota", [128, 2 * NODE_COLS])
        iota_b = sb("iota_b", [128, 2 * NODE_COLS], BF16)
        lane_i = sb("lane_i", [128, 1], I32)
        lane = sb("lane", [128, 1])
        earlier = sb("earlier", [128, 128], BF16)
        below = sb("below", [128, 128])
        ones = sb("ones", [128, 128])
        oh_lo = {d: sb(f"oh_lo_{d}", [EP, ET, 128], BF16) for d in "DS"}
        oh_hi = {d: sb(f"oh_hi_{d}", [EP, ET, tag[d].cols], BF16) for d in "DS"}
        oh_loT = {d: sb(f"oh_loT_{d}", [128, EDGES], BF16) for d in "DS"}
        same_or_place = sb("same_or_place", [EP, ET, 128], BF16)
        same = same_or_place[:, :, 0:EP]
        oh_pl = same_or_place
        in_tile = {d: sb(f"in_tile_{d}", [EP, ET]) for d in "DS"}
        found = {d: sb(f"found_{d}", [EP, ET]) for d in "DS"}
        junk = {d: sb(f"junk_{d}", [EP, tag[d].cols]) for d in "DS"}
        w_part = sb("w_part", [EP, 3, ET], BF16)
        w_rest = sb("w_rest", [EP, ET])
        total = {d: sb(f"total_{d}", [128, tag[d].cols]) for d in "DS"}
        runsum = {d: sb(f"runsum_{d}", [128, tag[d].cols]) for d in "DS"}
        start = {d: sb(f"start_{d}", [128, tag[d].cols]) for d in "DS"}
        table = {d: sb(f"table_{d}", [128, tag[d].cols]) for d in "DS"}
        table_hi = {d: sb(f"table_hi_{d}", [128, tag[d].cols], BF16) for d in "DS"}
        table_lo = {d: sb(f"table_lo_{d}", [128, tag[d].cols], BF16) for d in "DS"}
        pad_f = sb("pad_f", [128, 4])
        pad_i = sb("pad_i", [128, 4], I32)
        rank_i = sb("rank_i", [EP, ET], I32)
        rank_p = sb("rank_p", [EP, 2, ET], I32)
        rank_f = sb("rank_f", [EP, 2, ET])
        oh_ph = sb("oh_ph", [EP, ET, 41], BF16)
        value = sb("value", [EP, 3, ET])
        v_part = sb("v_part", [EP, 3, 3, ET], BF16)
        sorted_f = {d: sb(f"sorted_{d}", [128, 3, 41]) for d in "DS"}
        node_f = sb("node_f", [128, 5, NODE_COLS])
        degree = sb("degree", [128, NODE_COLS])
        mask = sb("mask", [128, 2 * NODE_COLS])
        rowsT = sb("rowsT", [128, 5, 128])
        idsT = {d: sb(f"idsT_{d}", [41, 128]) for d in "DS"}
        col0 = sb("col0", [128, 5])
        minus7 = sb("minus7", [1, 1])
        minus_half = sb("minus_half", [128, NODE_COLS])
        ones_wide = sb("ones_wide", [128, 2 * NODE_COLS])
        wide = [key_bc["D"][0:EP, :].bitcast(BF16)[:, 0:ET * 123].rearrange("p (t a c) -> p t a c", a=3, c=41),
                key_bc["D"][0:EP, :].bitcast(BF16)[:, ET * 123:2 * ET * 123].rearrange("p (t a c) -> p t a c", a=3, c=41),
                key_bc["S"][0:EP, :].bitcast(BF16)[:, 0:ET * 123].rearrange("p (t a c) -> p t a c", a=3, c=41)]
        weighted = [key_bc["S"][0:EP, :].bitcast(BF16)[:, m * ET * NODE_COLS:(m + 1) * ET * NODE_COLS]
                    .rearrange("p (t c) -> p t c", c=NODE_COLS) for m in range(3)]
        ids_f = {"D": low_bc[:, :].bitcast(F32), "S": key_bc["D"][:, :].bitcast(F32)}

        ps_edge = ctx.enter_context(nc.psum_tensor("ps_edge", [128, 512], F32))
        ps_tot = {d: ctx.enter_context(nc.psum_tensor(f"ps_tot_{d}", [128, 512], F32)) for d in "DS"}
        ps_run = {d: ctx.enter_context(nc.psum_tensor(f"ps_run_{d}", [128, 512], F32)) for d in "DS"}
        ps_look = {d: ctx.enter_context(nc.psum_tensor(f"ps_look_{d}", [128, 512], F32)) for d in "DS"}
        ps_sort = ctx.enter_context(nc.psum_tensor("ps_sort", [128, 512], F32))

        mix_banks = {"before": (ps_edge, ps_run["S"]), "after": (ps_edge, ps_tot["D"])}
        QUARTERS = 4
        K = BASES * QUARTERS
        CHUNK = 2048
        CHUNKS = DM // QUARTERS * DM // CHUNK
        TURNS = CHUNKS // 4
        bases = sb("bases", [K, 2, CHUNK])
        mixed = sb("mixed", [128, 2, 2, 512])
        factors = sb("factors", [K, 2, 32])
        factors_zeroed, factors_loaded = sem("factors_zeroed"), sem("factors_loaded")
        bases_loaded = [sem(f"bases_loaded{s}") for s in range(2)]
        mix_done, mix_copied = sem("mix_done"), sem("mix_copied")
        mix_stored = [sem(f"mix_stored{s}") for s in range(2)]

        raw_loaded, bc_loaded = sem("raw_loaded"), sem("bc_loaded")
        pool_made = sem("pool_made")
        dve_steps, pe_steps = sem("dve_steps"), sem("pe_steps")
        table_ready = {d: sem(f"table_ready_{d}") for d in "DS"}
        looked_up = {d: sem(f"looked_up_{d}") for d in "DS"}
        lookup_read = {d: sem(f"lookup_read_{d}") for d in "DS"}
        table_step = {d: sem(f"table_step_{d}") for d in "DS"}
        counted = {d: sem(f"counted_{d}") for d in "DS"}
        stored, reloaded, flags_loaded = sem("prep_stored"), sem("prep_reloaded"), sem("flags_loaded")
        mark = {}

        block = ctx.enter_context(nc.Block())

        @block.vector
        def _(dve):
            done = [0]

            def link(ins):
                done[0] += 1
                ins.then_inc(dve_steps, 1)
                dve.wait_ge(dve_steps, done[0])
                return done[0]

            def split(parts, rest, first):
                link(nc.vector.tensor_copy(parts[0], first))
                link(nc.vector.tensor_tensor(rest, first, parts[0], ALU.subtract))
                link(nc.vector.tensor_copy(parts[1], rest))
                return link(nc.vector.tensor_tensor(parts[2], rest, parts[1], ALU.subtract))

            link(nc.vector.memset(minus_half[:, :], -0.5))
            link(nc.vector.memset(ones_wide[:, :], 1.0))
            dve.wait_ge(pool_made, 6)
            link(nc.vector.tensor_copy(iota[:, :], iota_i[:, :]))
            link(nc.vector.tensor_copy(iota_b[:, :], iota_i[:, :]))
            link(nc.vector.tensor_copy(lane[:, :], lane_i[:, :]))
            link(nc.vector.tensor_scalar(earlier[:, :], iota[:, 0:128], lane[:, 0:1], None, ALU.is_lt))
            link(nc.vector.tensor_scalar(below[:, :], iota[:, 0:128], lane[:, 0:1], None, ALU.is_gt))
            dve.wait_ge(raw_loaded, 64)
            link(nc.vector.tensor_copy(raw_f[:, 0, :], raw_i[:, 1, :]))
            link(nc.vector.tensor_copy(raw_f[:, 3, :], raw_i[:, 0, :]))
            mark["raw rows"] = link(nc.vector.scalar_tensor_tensor(
                raw_f[:, 1, :], raw_i[:, 2, :], float(NODE_SPAN), raw_i[:, 0, :], ALU.mult, ALU.add))
            dve.wait_ge(pe_steps, 1)
            link(nc.vector.tensor_copy(edge[:, :, :], ps_edge[0:EP, 0:4 * ET].rearrange("p (a t) -> p a t", a=4)))
            link(nc.vector.tensor_copy(edge_i[:, :, :], edge[:, 0:2, :]))
            link(nc.vector.tensor_scalar(part_i[:, :, :], edge_i[:, :, :], 127, None, ALU.bitwise_and))
            link(nc.vector.tensor_copy(lo[:, :, :], part_i[:, :, :]))
            link(nc.vector.tensor_scalar(part_i[:, :, :], edge_i[:, :, :], 7, None, ALU.logical_shift_right))
            link(nc.vector.tensor_copy(hi[:, :, :], part_i[:, :, :]))
            split([w_part[:, n, :] for n in range(3)], w_rest[:, :], edge[:, 2, :])
            for n, d in enumerate("DS"):
                cols = tag[d].cols
                link(nc.vector.tensor_tensor(
                    oh_lo[d][:, :, :], iota[0:EP, 0:128].unsqueeze(1).broadcast_to([EP, ET, 128]),
                    lo[:, n, :].unsqueeze(2).broadcast_to([EP, ET, 128]), ALU.is_equal))
                mark["one-hots " + d] = link(nc.vector.tensor_tensor(
                    oh_hi[d][:, :, :], iota[0:EP, 0:cols].unsqueeze(1).broadcast_to([EP, ET, cols]),
                    hi[:, n, :].unsqueeze(2).broadcast_to([EP, ET, cols]), ALU.is_equal))
            dve.wait_ge(bc_loaded, 48)
            link(nc.vector.scalar_tensor_tensor(key_bc["S"][:, 0:EDGES], low_bc[:, 0:EDGES], float(NODE_SPAN), key_bc["S"][:, 0:EDGES],
                                                ALU.mult, ALU.add))
            for n, d in enumerate("DS"):
                link(nc.vector.tensor_scalar(low_bc[:, 0:EDGES], key_bc[d][:, 0:EDGES], 127, None, ALU.bitwise_and))
                mark["lookup one-hots " + d] = link(nc.vector.tensor_scalar(
                    oh_loT[d][:, :], low_bc[:, 0:EDGES], lane[:, 0:1], None, ALU.is_equal))
                link(nc.vector.tensor_tensor(
                    same[:, :, :], key_bc[d][0:EP, 0:EDGES].rearrange("p (t q) -> p t q", q=EP),
                    edge[:, n, :].unsqueeze(2).broadcast_to([EP, ET, EP]), ALU.is_equal))
                link(nc.vector.tensor_tensor(same[:, :, :], same[:, :, :],
                                             earlier[0:EP, 0:EP].unsqueeze(1).broadcast_to([EP, ET, EP]), ALU.mult))
                link(nc.vector.reduce_sum(in_tile[d][:, :], same[:, :, :], AX.X))

            dve.wait_ge(pe_steps, 3)
            for d in "DS":
                cols = tag[d].cols
                link(nc.vector.tensor_copy(total[d][:, :], ps_tot[d][:, 0:cols]))
                link(nc.vector.tensor_tensor_scan(runsum[d][:, :], ones_wide[:, 0:cols], total[d][:, :], 0.0,
                                                  ALU.mult, ALU.add))
                mark["prefix " + d] = link(nc.vector.tensor_tensor(
                    runsum[d][:, :], runsum[d][:, :], total[d][:, :], ALU.subtract))
            dve.wait_ge(pe_steps, 5)
            link(nc.vector.tensor_copy(start["D"][:, :], ps_tot["D"][:, 0:NODE_COLS]))
            link(nc.vector.tensor_copy(start["S"][:, :], ps_tot["S"][:, 0:2 * NODE_COLS]))
            link(nc.vector.tensor_copy(pad_i[:, 0:1], ps_sort[:, 0:1]))
            link(nc.vector.tensor_scalar(pad_f[:, 0:1], ps_sort[:, 0:1], -1.0, None, ALU.mult))
            link(nc.vector.tensor_copy(pad_i[:, 1:2], pad_f[:, 0:1]))
            link(nc.vector.tensor_scalar(pad_i[:, 2:3], pad_i[:, 1:2], 127, None, ALU.bitwise_and))
            link(nc.vector.tensor_copy(pad_f[:, 1:2], pad_i[:, 2:3]))
            link(nc.vector.tensor_tensor(pad_f[:, 2:3], pad_f[:, 1:2], ps_sort[:, 0:1], ALU.add))
            link(nc.vector.tensor_scalar(pad_f[:, 3:4], pad_f[:, 2:3], 1.0 / 128, None, ALU.mult))
            link(nc.vector.tensor_copy(P.type0_tiles[:, :], pad_f[:, 3:4]))
            link(nc.vector.tensor_scalar(P.is_type0[:, :], iota[:, 0:P.S.tiles], pad_f[:, 3:4], None, ALU.is_lt))
            link(nc.vector.tensor_scalar(start["S"][:, NODE_COLS:], start["S"][:, NODE_COLS:], pad_f[:, 1:2],
                                         None, ALU.add))

            def advance(d, t, first):
                cols = tag[d].cols
                if first:
                    nc.vector.tensor_copy(table[d][:, :], start[d][:, :]).then_inc(table_step[d], 1)
                else:
                    dve.wait_ge(counted[d], t)
                    nc.vector.tensor_tensor(table[d][:, :], ps_run[d][:, 0:cols], start[d][:, :], ALU.add)\
                        .then_inc(table_step[d], 1)

            def halve(d, t, first):
                if not first:
                    dve.wait_ge(looked_up[d], t)
                dve.wait_ge(table_step[d], 2 * t + 1)
                nc.vector.tensor_copy(table_hi[d][:, :], table[d][:, :]).then_inc(table_step[d], 1)

            def rest(d, t):
                dve.wait_ge(table_step[d], 2 * t + 2)
                nc.vector.tensor_tensor(table_lo[d][:, :], table[d][:, :], table_hi[d][:, :], ALU.subtract)\
                    .then_inc(table_ready[d], 1)

            def pick(d, t):
                dve.wait_ge(looked_up[d], t + 1)
                if not isinstance(t, int) or t > 0:
                    dve.wait_ge(lookup_read[d], t)
                nc.vector.scalar_tensor_tensor(
                    junk[d][:, :], ps_look[d][0:EP, 0:tag[d].cols], 1.0,
                    oh_hi[d][:, bass.ds(t, 1), :].rearrange("p a c -> p (a c)"), ALU.mult, ALU.mult,
                    accum_out=found[d][:, bass.ds(t, 1)]).then_inc(lookup_read[d], 1)

            def place(t, first):
                for d in "DS":
                    advance(d, t, first)
                for d in "DS":
                    halve(d, t, first)
                for d in "DS":
                    rest(d, t)
                for d in "DS":
                    pick(d, t)

            place(0, True)
            with dve.Fori(1, ET) as t:
                place(t, False)
            dve.wait_ge(lookup_read["D"], ET)
            dve.wait_ge(lookup_read["S"], ET)

            for d in "DS":
                cols = tag[d].cols
                link(nc.vector.tensor_tensor(rank_i[:, :], found[d][:, :], in_tile[d][:, :], ALU.add))
                link(nc.vector.tensor_scalar(rank_p[:, 0, :], rank_i[:, :], 127, None, ALU.bitwise_and))
                link(nc.vector.tensor_scalar(rank_p[:, 1, :], rank_i[:, :], 7, None, ALU.logical_shift_right))
                link(nc.vector.tensor_copy(rank_f[:, :, :], rank_p[:, :, :]))
                if d == "S":
                    dve.wait_ge(pe_steps, 6)
                link(nc.vector.tensor_tensor(
                    oh_pl[:, :, :], iota[0:EP, 0:128].unsqueeze(1).broadcast_to([EP, ET, 128]),
                    rank_f[:, 0, :].unsqueeze(2).broadcast_to([EP, ET, 128]), ALU.is_equal))
                link(nc.vector.tensor_tensor(
                    oh_ph[:, :, :], iota[0:EP, 0:41].unsqueeze(1).broadcast_to([EP, ET, 41]),
                    rank_f[:, 1, :].unsqueeze(2).broadcast_to([EP, ET, 41]), ALU.is_equal))
                link(nc.vector.tensor_scalar(value[:, 0, :], edge[:, 0 if d == "D" else 1, :], 1.0, None, ALU.add))
                link(nc.vector.tensor_scalar(value[:, 1, :], edge[:, 3 if d == "D" else 0, :], 1.0, None, ALU.add))
                link(nc.vector.tensor_copy(value[:, 2, :], edge[:, 2, :]))
                for n in range(3):
                    split([v_part[:, m, n, :] for m in range(3)], w_rest[:, :], value[:, n, :])
                for m in range(3):
                    for n in range(3):
                        step = link(nc.vector.tensor_tensor(
                            wide[m][:, :, n, :], oh_ph[:, :, :],
                            v_part[:, m, n, :].unsqueeze(2).broadcast_to([EP, ET, 41]), ALU.mult))
                mark["ordering operands " + d] = step
                dve.wait_ge(pe_steps, 6 if d == "D" else 7)
                link(nc.vector.tensor_copy(sorted_f[d][:, :, :],
                                           ps_sort[:, 0:123].rearrange("p (a c) -> p a c", a=3)))
                tiles = tag[d].tiles
                link(nc.vector.tensor_scalar(tag[d].gather[:, :], sorted_f[d][:, 1, 0:tiles], -1.0, 0.0,
                                             ALU.add, ALU.max))
                if d == "D":
                    link(nc.vector.tensor_scalar(P.receivers[:, :], sorted_f[d][:, 0, 0:tiles], -1.0, 0.0,
                                                 ALU.add, ALU.max))
                    link(nc.vector.tensor_copy(P.weights[:, :], sorted_f[d][:, 2, 0:tiles]))
                mark["sorted " + d] = done[0]

            for m in range(3):
                mark["weighted one-hots"] = link(nc.vector.tensor_tensor(
                    weighted[m], oh_hi["D"][:, :, :], w_part[:, m, :].unsqueeze(2).broadcast_to([EP, ET, NODE_COLS]),
                    ALU.mult))

            for d, rows in (("D", [0]), ("S", [1, 2])):
                cols = tag[d].cols
                link(nc.vector.tensor_scalar(mask[:, 0:cols], total[d][:, :], 0.0, float(NO_ROW), ALU.is_equal, ALU.mult))
                link(nc.vector.scalar_tensor_tensor(table["S"][:, 0:cols], total[d][:, :], -1.0, start[d][:, :],
                                                    ALU.add, ALU.add))
                link(nc.vector.tensor_tensor(
                    node_f[:, rows[0]:rows[-1] + 1, :].rearrange("p a c -> p (a c)"), table["S"][:, 0:cols],
                    mask[:, 0:cols], ALU.add))
            dve.wait_ge(pe_steps, 8)
            link(nc.vector.tensor_scalar(degree[:, :], ps_edge[:, 0:NODE_COLS], 1.0, None, ALU.add))
            link(nc.vector.tensor_scalar(mask[:, 0:NODE_COLS], degree[:, :], 0.0, None, ALU.is_gt))
            mark["degree clamped"] = link(nc.vector.tensor_scalar(degree[:, :], degree[:, :], 1e-30, None, ALU.max))
            dve.wait_ge(pool_made, 7)
            link(nc.vector.tensor_tensor(node_f[:, 3, :], degree[:, :], mask[:, 0:NODE_COLS], ALU.mult))
            link(nc.vector.tensor_scalar(mask[:, 0:NODE_COLS], total["D"][:, :], 1.0, None, ALU.max))
            mark["node tables"] = link(nc.vector.reciprocal(node_f[:, 4, :], mask[:, 0:NODE_COLS]))
            dve.wait_ge(pe_steps, 9)
            link(nc.vector.tensor_copy(rowsT[0:NODE_COLS, :, :].rearrange("p a c -> p (a c)")[:, 0:512],
                                       ps_tot["D"][0:NODE_COLS, :]))
            link(nc.vector.tensor_copy(rowsT[0:NODE_COLS, 4, :], ps_tot["S"][0:NODE_COLS, 0:128]))
            link(nc.vector.tensor_copy(idsT["D"][0:40, :], ps_tot["S"][0:40, 128:256]))
            mark["transposed"] = link(nc.vector.tensor_copy(idsT["S"][:, :], ps_tot["S"][0:41, 256:384]))
            dve.wait_ge(reloaded, 80)
            for n, out in enumerate((P.last_D, P.last_S0, P.last_S1, P.dinv, P.rdeg)):
                link(nc.vector.tensor_copy(out[:, 0:1], col0[:, n:n + 1]))
                link(nc.vector.tensor_copy(out[:, 1:NODE_STEPS], node_f[:, n, 0:NODE_STEPS - 1]))
            for d in "DS":
                m = tag[d].tiles * 128
                dve.wait_ge(flags_loaded, 32)
                ids = ids_f[d]
                link(nc.vector.tensor_tensor(tag[d].same_run[:, 0:m], ids[:, 1:m + 1], ids[:, 0:m], ALU.is_equal))
                link(nc.vector.memset(tag[d].same_run[:, m:m + 1], 0.0))

        @block.scalar
        def _(act):
            act.wait_ge(factors_zeroed, 1)
            with nc.allow_non_contiguous_dma(reason="60 coefficients a layer"):
                for layer in range(2):
                    for q in range(QUARTERS):
                        for rel in range(RELATIONS):
                            at = QUARTERS * rel + q
                            act.dma_start(factors[q:K:QUARTERS, layer, at:at + 1],
                                          att[layer][rel:rel + 1, :].rearrange("a b -> b a")).then_inc(factors_loaded, 16)

            for layer in range(2):
                view = mixed_w[layer].rearrange("m (q c j n) -> m q c j n", c=2, j=4, n=512)

                def keep_chunks(i, when, layer=layer, view=view):
                    turn = layer * TURNS + i
                    for slot in range(2):
                        if not isinstance(i, int) or i:
                            act.wait_ge(mix_stored[slot], 64 * turn)
                        for c in range(2):
                            act.wait_ge(mix_done, 4 * turn + (2 * slot + c + 1))
                            nc.scalar.activation(mixed[:, slot, c, :], mix_banks[when][c][:, :], ACT.Copy).then_inc(mix_copied, 1)
                        act.wait_ge(mix_copied, 4 * turn + (2 * slot + 2))
                        for j in range(4):
                            to = view[:, bass.ds(2 * i + slot, 1), :, j, :].rearrange("m a c n -> m (a c) n")
                            act.dma_start(to, mixed[32 * j:32 * j + RELATIONS * QUARTERS, slot, :, :])\
                                .then_inc(mix_stored[slot], 16)
                if layer == 0:
                    for i in range(MIX_PLACE // 4):
                        keep_chunks(i, "before")
                with act.Fori(0 if layer else MIX_PLACE // 4, TURNS) as i:
                    keep_chunks(i, "after")
            for slot in range(2):
                act.wait_ge(mix_stored[slot], 64 * 2 * TURNS)

        @block.gpsimd
        def _(pool):
            nc.gpsimd.memset(factors[:, :, :], 0.0).then_inc(factors_zeroed, 1)
            nc.gpsimd.iota(iota_i[:, :], pattern=[[1, 2 * NODE_COLS]], base=0, channel_multiplier=0).then_inc(pool_made, 1)
            nc.gpsimd.iota(lane_i[:, :], pattern=[[0, 1]], base=0, channel_multiplier=1).then_inc(pool_made, 1)
            nc.gpsimd.memset(ones[:, :], 1.0).then_inc(pool_made, 1)
            nc.gpsimd.memset(minus7[:, :], -7.0).then_inc(pool_made, 1)
            nc.gpsimd.memset(P.ident[:, :], 0.0).then_inc(pool_made, 1)
            pool.wait_ge(pool_made, 5)
            nc.gpsimd.affine_select(out=P.ident[:, :], in_=P.ident[:, :], compare_op=ALU.not_equal, fill=1.0,
                                    base=0, pattern=[[-1, 128]], channel_multiplier=1).then_inc(pool_made, 1)
            pool.wait_ge(dve_steps, mark["degree clamped"])
            nc.gpsimd.tensor_tensor(degree[:, :], degree[:, :], minus_half[:, :], ALU.pow).then_inc(pool_made, 1)

        @block.tensor
        def _(pe):
            def mix(k, s):
                layer = 0 if k < CHUNKS else 1
                pe.wait_ge(bases_loaded[s], 16 * (k // 2 + 1))
                if k >= 2:
                    pe.wait_ge(mix_copied, k - 1)
                mix_products(layer, s, "before" if k < MIX_PLACE else "after")

            def mix_products(layer, s, when):
                for j in range(4):
                    last = nc.tensor.matmul(mix_banks[when][s][32 * j:32 * j + 32, :], factors[:, layer, :],
                                            bases[:, s, j * 512:(j + 1) * 512], start=True, stop=True)
                last.then_inc(mix_done, 1)

            pe.wait_ge(dve_steps, mark["raw rows"])
            for n in range(4):
                last = nc.tensor.transpose(ps_edge[0:EP, n * ET:(n + 1) * ET], raw_f[:, n, :], P.ident[0:ET, 0:ET])
            last.then_inc(pe_steps, 1)
            pe.wait_ge(factors_loaded, 2 * QUARTERS * RELATIONS * 16)
            for d in "DS":
                cols = tag[d].cols
                pe.wait_ge(dve_steps, mark["one-hots " + d])

                def count(t, begin, end):
                    return nc.tensor.matmul(ps_tot[d][:, 0:cols], oh_lo[d][:, bass.ds(t, 1), :].rearrange("p a c -> p (a c)"),
                                            oh_hi[d][:, bass.ds(t, 1), :].rearrange("p a c -> p (a c)"),
                                            start=begin, stop=end, skip_group_check=True)
                over_columns(pe, count).then_inc(pe_steps, 1)
                if d == "D":
                    for k in range(MIX_D):
                        mix(k, k % 2)
            for d in "DS":
                cols = tag[d].cols
                pe.wait_ge(dve_steps, mark["prefix S"])
                nc.tensor.matmul(ps_tot[d][:, 0:cols], below[:, :], total[d][:, :], start=True, stop=False)
                last = nc.tensor.matmul(ps_tot[d][:, 0:cols], ones[:, :], runsum[d][:, :], start=False, stop=True)
                if d == "D":
                    last.then_inc(pe_steps, 1)
            nc.tensor.matmul(ps_sort[:, 0:1], ones[:, :], runsum["S"][:, NODE_COLS:NODE_COLS + 1], start=True, stop=True)\
                .then_inc(pe_steps, 1)
            for k in range(MIX_D, MIX_PLACE):
                mix(k, k % 2)

            def look_up(d, t, first):
                if not first:
                    pe.wait_ge(lookup_read[d], t)
                pe.wait_ge(table_ready[d], t + 1)
                cols = tag[d].cols
                one_hot = oh_loT[d][:, bass.ds(t * EP, EP)]
                nc.tensor.matmul(ps_look[d][0:EP, 0:cols], one_hot, table_hi[d][:, :], start=True, stop=False)
                nc.tensor.matmul(ps_look[d][0:EP, 0:cols], one_hot, table_lo[d][:, :], start=False, stop=True)\
                    .then_inc(looked_up[d], 1)

            def count_on(d, t, first):
                nc.tensor.matmul(ps_run[d][:, 0:tag[d].cols], oh_lo[d][:, bass.ds(t, 1), :].rearrange("p a c -> p (a c)"),
                                 oh_hi[d][:, bass.ds(t, 1), :].rearrange("p a c -> p (a c)"),
                                 start=first, stop=True, skip_group_check=True).then_inc(counted[d], 1)

            pe.wait_ge(mix_copied, MIX_PLACE)
            for d in "DS":
                look_up(d, 0, True)
                count_on(d, 0, True)
            for layer, first_t, turns in ((0, 1, (CHUNKS - MIX_PLACE) // 2),
                                          (1, 1 + CHUNKS - MIX_PLACE, (ET - 2 - (CHUNKS - MIX_PLACE)) // 2)):
                with pe.Fori(0, turns) as i:
                    for m in range(2):
                        t = 2 * i + (first_t + m)
                        for d in "DS":
                            look_up(d, t, False)
                            count_on(d, t, False)
                        k = MIX_PLACE + first_t - 1 + m
                        pe.wait_ge(bases_loaded[k % 2], 16 * i + 16 * (k // 2 + 1))
                        pe.wait_ge(mix_copied, 2 * i + (k - 1))
                        mix_products(layer, k % 2, "after")
            for d in "DS":
                look_up(d, ET - 1, False)
                count_on(d, ET - 1, False)
            placed = MIX_PLACE + ET - 2
            half_way = (placed + 2 * CHUNKS) // 2
            for k in range(placed, half_way):
                mix(k, k % 2)

            for d in "DS":
                if d == "S":
                    for k in range(half_way, 2 * CHUNKS):
                        mix(k, k % 2)
                pe.wait_ge(dve_steps, mark["ordering operands " + d])
                if d == "S":
                    pe.wait_ge(dve_steps, mark["sorted D"])

                def order(t, begin, end):
                    for m in range(3):
                        last = nc.tensor.matmul(ps_sort[:, 0:123], oh_pl[:, bass.ds(t, 1), :].rearrange("p a c -> p (a c)"),
                                                wide[m][:, bass.ds(t, 1), :, :].rearrange("p b a c -> p (b a c)"),
                                                start=begin and m == 0, stop=end and m == 2, skip_group_check=True)
                    return last
                over_columns(pe, order).then_inc(pe_steps, 1)
            pe.wait_ge(dve_steps, mark["weighted one-hots"])
            pe.wait_ge(mix_copied, 2 * CHUNKS)

            def weigh(t, begin, end):
                for m in range(3):
                    last = nc.tensor.matmul(ps_edge[:, 0:NODE_COLS], oh_lo["D"][:, bass.ds(t, 1), :].rearrange("p a c -> p (a c)"),
                                            weighted[m][:, bass.ds(t, 1), :].rearrange("p a c -> p (a c)"),
                                            start=begin and m == 0, stop=end and m == 2, skip_group_check=True)
                return last
            over_columns(pe, weigh).then_inc(pe_steps, 1)
            pe.wait_ge(dve_steps, mark["node tables"])
            for n in range(5):
                out = ps_tot["D"][0:NODE_COLS, n * 128:(n + 1) * 128] if n < 4 else ps_tot["S"][0:NODE_COLS, 0:128]
                nc.tensor.transpose(out, node_f[:, n, :], P.ident[:, :])
            nc.tensor.transpose(ps_tot["S"][0:40, 128:256], sorted_f["D"][:, 0, 0:40], P.ident[:, :])
            nc.tensor.transpose(ps_tot["S"][0:41, 256:384], sorted_f["S"][:, 0, 0:41], P.ident[:, :]).then_inc(pe_steps, 1)

        @block.sync
        def _(sp):
            for n, a in enumerate((src, dst, edge_type)):
                sp.dma_start(raw_i[:, n, :], a.rearrange("(t p) -> t p", p=EP)).then_inc(raw_loaded, 16)
            sp.dma_start(raw_f[:, 2, :], edge_weight.rearrange("(t p) -> t p", p=EP)).then_inc(raw_loaded, 16)
            for a, out in ((dst, key_bc["D"]), (src, key_bc["S"]), (edge_type, low_bc)):
                sp.dma_start(out[:, 0:EDGES], a.partition_broadcast(128)).then_inc(bc_loaded, 16)
            for layer in range(2):
                view = basis[layer].rearrange("b (s i) o -> (b s) (i o)", s=QUARTERS)

                def load_chunks(i, layer=layer, view=view):
                    for m in range(2):
                        k = layer * CHUNKS + m + 2 * i
                        if not isinstance(i, int) or layer:
                            sp.wait_ge(mix_done, k - 1)
                        sp.dma_start(bases[:, m, :], view[:, bass.ds((m + 2 * i) * CHUNK, CHUNK)])\
                            .then_inc(bases_loaded[m], 16)
                if layer == 0:
                    load_chunks(0)
                with sp.Fori(1 - layer, CHUNKS // 2) as i:
                    load_chunks(i)
            sp.wait_ge(dve_steps, mark["transposed"])
            for n in range(5):
                sp.dma_start(pos_dram[n].rearrange("(h l) -> h l", l=128), rowsT[0:NODE_COLS, n, :]).then_inc(stored, 16)
            for d in "DS":
                sp.dma_start(seg_dram[d][1:].rearrange("(h l) -> h l", l=128), idsT[d][0:tag[d].tiles, :])\
                    .then_inc(stored, 16)
                sp.dma_start(seg_dram[d][0:1].rearrange("(a n) -> a n", a=1), minus7[:, :]).then_inc(stored, 16)
            sp.wait_ge(stored, 9 * 16)
            for n in range(5):
                sp.dma_start(col0[:, n:n + 1], pos_dram[n][N - 128:N].rearrange("(p a) -> p a", a=1)).then_inc(reloaded, 16)
            for d in "DS":
                m = tag[d].tiles * 128 + 1
                sp.dma_start(ids_f[d][:, 0:m], seg_dram[d].partition_broadcast(128)).then_inc(flags_loaded, 16)



class Named:
    pass


class Ordering:

    def __init__(self, tiles, cols, gather, same_run):
        self.tiles, self.cols, self.gather, self.same_run = tiles, cols, gather, same_run


class Step:

    def __init__(self, c, i=None):
        self.c, self.i = c, i

    def number(self, first=0, each=1):
        return first + each * self.c if self.i is None else first + each * self.c + 4 * each * self.i

    def quarter(self, first, each=16):
        k = (first + self.c) // 4 + 1
        return each * k if self.i is None else each * k + each * self.i

    @property
    def t(self):
        return self.number()

    def back(self, k):
        return Step(self.c - k, self.i)


def pipelined(eng, n, *stages):
    lag = max(l for l, _ in stages)
    head = lag + 4 + (n - lag) % 4
    for j in range(head):
        for l, stage in stages:
            if j >= l:
                stage(Step(j - l))
    with eng.Fori(0, (n - head) // 4) as i:
        for s in range(4):
            for l, stage in stages:
                stage(Step(head + s - l, i))
    for j in range(n, n + lag):
        for l, stage in stages:
            if j - l < n:
                stage(Step(j - l))


PASSES = {"N1": NODE_STEPS, "E1": D_TILES, "N2": NODE_STEPS, "E2": D_TILES, "N3": NODE_STEPS,
          "E3": S_TILES, "N4": NODE_STEPS, "E4": S_TILES, "N5": NODE_STEPS, "E5": D_TILES,
          "E6": D_TILES, "N6": NODE_STEPS, "E7": D_TILES, "N7": NODE_STEPS}
DENSE = ("N1", "N3", "E3", "N4", "E4", "N5", "E5", "E6", "E7", "N7")
TRANSPOSED = ("N1", "E1", "E2", "N3", "E3", "N4", "E4", "N5", "E5", "E6", "E7", "N7")
SCANNED = ("E1", "E2", "E3", "E4", "E6", "E7")
GATHERS = ("N2", "N3", "N4", "N5", "N6", "N7")
GATHERED = ("E1", "E2", "E3", "E4", "E5", "E7")
LOADED = tuple(p for p in PASSES if p not in GATHERED)
LISTED = ("N2", "N4")
RESIDUAL = {"N3": 0, "N5": 0, "N7": 2}
NORMED = ("N3", "N5", "N6", "N7")


class Tally:

    def __init__(self, sem, passes, credit=0):
        self.sem, self.credit, self.first, self.last, at = sem, credit, {}, {}, 0
        for p, n in PASSES.items():
            self.first[p] = at
            at += n if p in passes else 0
            self.last[p] = at

    def done(self, p, step):
        return self.sem, step.number(self.credit + self.first[p] + 1)

    def free(self, p, step, depth):
        return self.sem, step.number(self.credit + self.first[p] + 1 - depth)

    def through(self, p):
        return self.sem, self.credit + self.last[p]


class Ring:

    def __init__(self, sems, passes, credit=0):
        self.sems, self.credit, self.first, at = sems, credit, {}, 0
        for p, n in PASSES.items():
            self.first[p] = at
            at += n if p in passes else 0
        self.passes, self.total = passes, at

    def slot(self, p, step):
        return (self.first[p] + step.c) % 4

    def sem(self, p, step):
        return self.sems[self.slot(p, step)]

    def done(self, p, step):
        return self.sem(p, step), step.quarter(self.first[p])

    def free(self, p, step):
        return self.sem(p, step), step.quarter(self.first[p])

    def through(self, p):
        n = self.first[p] + (PASSES[p] if p in self.passes else 0)
        return [(self.sems[s], self.credit + 16 * len(range(s, n, 4))) for s in range(4)]


def layers_block(nc, P, x, out, par, drams):
    X = drams
    ctx = ExitStack()
    with ctx:
        def sb(name, shape, dt=F32):
            return ctx.enter_context(nc.sbuf_tensor(name, shape, dt))

        def sem(name):
            return ctx.enter_context(nc.semaphore(name))

        rows = sb("rows", [128, 5, 4, DM])
        xin, agg, agg2, res, outs = (rows[:, n, :, :] for n in range(5))
        y = sb("y", [128, 4, DM])
        scan = sb("scan", [128, 2, DM])
        xT_hi, xT_lo = sb("xT_hi", [128, 2, DM], F32R), sb("xT_lo", [128, 2, DM], F32R)
        rT_hi, rT_lo = sb("rT_hi", [128, 2, DM], F32R), sb("rT_lo", [128, 2, DM], F32R)
        we_hi, we_lo = sb("we_hi", [128, 3, 4, DM], F32R), sb("we_lo", [128, 3, 4, DM], F32R)
        wn_hi, wn_lo = sb("wn_hi", [128, 4, DM], F32R), sb("wn_lo", [128, 4, DM], F32R)
        staged = sb("staged", [128, 2, 4 * DM])
        b1 = sb("b1", [128, DH])
        b2, bias1, bias2, bff, b3 = (sb(n, [128, DM]) for n in ("b2", "bias1", "bias2", "bff", "b3"))
        bqkv = res[:, 0:3, :]
        gate = agg2[:, 0:RELATIONS, :]
        prod = sb("prod", [128, DM])
        srow = sb("srow", [HEADS, D_TILES * 128])
        scores = sb("scores", [128, 2, HEADS])
        att = sb("att", [HEADS, 2, 128])
        list_col = [sb(f"list_col{n}", [128, 4], I32) for n in range(2)]
        z = sb("z", [128, 4])
        g = sb("g", [128, 4])
        sq = sb("sq", [128, 4])
        rn = sb("rn", [128, 4])
        stats = sb("stats", [128, 4, 6])
        mv = sb("mv", [128, 4, 2])
        ve = sb("ve", [128, 4])
        zero = sb("zero", [128, 1])
        half = sb("half", [128, 1])
        rstd = sb("rstd", [128, 4])
        nb = sb("nb", [128, 4])
        pT = ctx.enter_context(nc.psum_tensor("pT", [128, 2, DM], F32))
        pM = ctx.enter_context(nc.psum_tensor("pM", [128, 6, DM], F32))

        loaded = Ring([sem(f"loaded{s}") for s in range(4)], LOADED)
        gathered = Ring([sem(f"gathered{s}") for s in range(4)], GATHERED)
        agg_in = Ring([sem(f"agg_in{s}") for s in range(4)], GATHERS + ("E5",))
        agg2_in = Ring([sem(f"agg2_in{s}") for s in range(4)], ("N4", "N5"))
        res_in = Ring([sem(f"res_in{s}") for s in range(4)], RESIDUAL)
        stored = Ring([sem(f"stored{s}") for s in range(4)], PASSES, credit=16)
        list_copied = Tally(sem("list_copied"), [p for p in GATHERS + GATHERED if p not in LISTED])
        list_copied2 = Tally(sem("list_copied2"), ("N5", "E5"))
        listed = Tally(sem("listed"), LISTED)
        listed2 = Tally(sem("listed2"), ("N4",))
        prefilled = Tally(sem("prefilled"), ("N3", "N7"))
        prefilled2 = Tally(sem("prefilled2"), ("N5",))
        bias_filled = Tally(sem("bias_filled"), ("N5", "N6"))
        transposed = Tally(sem("transposed"), TRANSPOSED)
        high = Tally(sem("high"), DENSE)
        split = Tally(sem("split"), DENSE)
        scanned = Tally(sem("scanned"), SCANNED)
        scaled = Tally(sem("scaled"), ("E1", "E2", "E3", "E4", "E6"))
        gated = Tally(sem("gated"), ("E3", "E4"))
        sigmoid = Tally(sem("sigmoid"), ("E3", "E4"))
        summed = Tally(sem("summed"), ("N2", "N3", "N6"))
        product = Tally(sem("product"), TRANSPOSED, credit=2)
        evacuated = Tally(sem("evacuated"), [p for p in TRANSPOSED if p != "E5"], credit=2)
        added = Tally(sem("added"), ("N2", "N4", "N5"))
        squared = Tally(sem("squared"), ("N3",))
        bounded = Tally(sem("bounded"), ("N3",))
        inv_norm = Tally(sem("inv_norm"), ("N3",))
        silued = Tally(sem("silued"), ("N7",))
        biased = Tally(sem("biased"), ("N7",))
        y_ready = Tally(sem("y_ready"), ("N3", "N5", "N7"))
        bn_done = Tally(sem("bn_done"), NORMED)
        mean_ready = Tally(sem("mean_ready"), NORMED)
        var_ready = Tally(sem("var_ready"), NORMED)
        rstd_ready = Tally(sem("rstd_ready"), NORMED)
        shift_ready = Tally(sem("shift_ready"), NORMED)
        finished = Tally(sem("finished"), ("N2", "N3", "N4", "N5", "N6", "N7"), credit=4)
        scored = Tally(sem("scored"), ("E5",))
        score_T = Tally(sem("score_T"), ("E5",))
        score_kept = Tally(sem("score_kept"), ("E5",))
        qk_added = Tally(sem("qk_added"), ("E5",))
        v_done = Tally(sem("v_done"), ("E5",))
        v_added = Tally(sem("v_added"), ("E5",))
        multiplied = Tally(sem("multiplied"), ("E5",))
        att_cut = Tally(sem("att_cut"), ("E6",))
        att_T = Tally(sem("att_T"), ("E6",))
        softmax = sem("softmax")
        exps = sem("exps")
        w_loaded = [sem(f"w_loaded{s}") for s in range(2)]
        w_high, w_low = sem("w_high"), sem("w_low")
        consts_loaded, half_set, zero_set = sem("consts_loaded"), sem("half_set"), sem("zero_set")
        settled = sem("settled")

        def wait(eng, pair):
            eng.wait_ge(pair[0], pair[1])

        def wait_all(eng, pairs):
            for pair in pairs:
                wait(eng, pair)

        def xin_in(p):
            return loaded if p in LOADED else gathered

        def settle(eng):
            eng.sem_inc(settled, 1)

        def col(table, step):
            return table[:, bass.ds(step.t, 1)]

        def node_rows(array, step):
            return array[N - 128:N, :] if step.i is None and step.c == 0 else \
                array[bass.ds(step.number(-128, 128), 128), :]

        def edge_rows(array, step):
            return array[bass.ds(step.number(0, 128), 128), :]

        def halves(place):
            return (wn_hi[:, :, :], wn_lo[:, :, :]) if place == "n" else (we_hi[:, place, :, :], we_lo[:, place, :, :])

        def square(a):
            return a.rearrange("(k p) n -> p k n", p=128)

        def relation(l, r):
            return X.mixed[l].rearrange("(r s) (i o) -> r i s o", r=RELATIONS, o=DM)[r]

        NAMES = list(PASSES)
        WEIGHTS = [("N1", "n", square(par.W1), DM // 128, DH, None),
                   ("E1", "n", square(par.W2), DH // 128, DM, "N1"),
                   ("N2", 0, relation(0, 0), 4, DM, None), ("E2", 1, relation(0, 1), 4, DM, None),
                   ("N3", 2, square(par.W_qkv[:, 2 * DM:]), 4, DM, None),
                   ("E3", "n", square(par.root1), 4, DM, "N3"),
                   ("N4", 0, relation(1, 0), 4, DM, "E3"), ("N4", 1, relation(1, 1), 4, DM, "E3"),
                   ("E4", "n", square(par.root2), 4, DM, "N4"),
                   ("N5", 0, square(par.W_qkv[:, 0:DM]), 4, DM, "E4"),
                   ("N5", 1, square(par.W_qkv[:, DM:2 * DM]), 4, DM, "E4"),
                   ("E5", "n", square(par.W_ff), 4, DM, "N5"),
                   ("N6", 0, square(par.W_l), 4, DM, "E5"), ("N6", 1, square(par.W_r), 4, DM, "E5")]

        def staging(n):
            k, width = WEIGHTS[n][3:5]
            return staged[:, n % 2, 0:k * width].rearrange("p (k n) -> p k n", k=k)

        def weights_before(p):
            return [(n, w) for n, w in enumerate(WEIGHTS) if w[0] == p]

        WEIGHTS_USED = {"N1": 1, "E1": 1, "E2": 1, "N3": 2, "E3": 4, "N4": 6, "E4": 8, "N5": 9, "E5": 11, "E6": 12,
                        "E7": 13, "N7": 14}

        def need_weights(pe, count):
            pe.wait_ge(w_low, count)

        def load_weights(sp, p):
            at = NAMES.index(p)
            upto = min(len(WEIGHTS), 2 + sum(NAMES.index(w[0]) <= at for w in WEIGHTS))
            done = 0 if not at else min(len(WEIGHTS), 2 + sum(NAMES.index(w[0]) < at for w in WEIGHTS))
            for n in range(done, upto):
                if n >= 2:
                    sp.wait_ge(w_low, n - 1)
                sp.dma_start(staging(n), WEIGHTS[n][2]).then_inc(w_loaded[n % 2], 16)

        def split_weights_high(act, p):
            for n, (_, place, _, k, width, after) in weights_before(p):
                act.wait_ge(w_loaded[n % 2], 16 * (n // 2 + 1))
                if after:
                    wait(act, product.through(after))
                src = staging(n)
                nc.scalar.activation(halves(place)[0][:, 0:k, 0:width], src, ACT.Copy).then_inc(w_high, 1)

        def split_weights_low(dve, p):
            for n, (_, place, _, k, width, after) in weights_before(p):
                dve.wait_ge(w_high, n + 1)
                src = staging(n)
                hi, lo = halves(place)
                nc.vector.tensor_tensor(lo[:, 0:k, 0:width], src, hi[:, 0:k, 0:width].bitcast(F32), ALU.subtract)\
                    .then_inc(w_low, 1)

        XIN_USED = {"N1": transposed, "E1": scaled, "N2": summed, "E2": scaled, "N3": summed, "E3": scaled,
                    "N4": transposed, "E4": scaled, "N5": transposed, "E5": transposed, "E6": scaled,
                    "N6": summed, "E7": transposed, "N7": transposed}
        PT_USED = {p: scanned if p in SCANNED else split for p in TRANSPOSED}
        AGG_USED = {"N2": summed, "N3": summed, "N4": evacuated, "N5": evacuated, "E5": transposed,
                    "N6": summed, "N7": silued}
        OUT_FILLED = {p: evacuated if p in ("N1", "E1", "E2", "E3", "E4", "E6", "E7") else
                      v_added if p == "E5" else finished for p in PASSES}
        STORES = {"N1": X.h, "E1": X.r1, "N2": X.g, "E2": X.r2, "N3": X.x1, "E3": X.r3, "N4": X.hb, "E4": X.r4,
                  "N5": X.x2, "E5": X.v, "E6": X.r5, "N6": X.x3, "E7": X.r6, "N7": out}
        LOADS = {"N1": x, "N2": X.h, "N3": X.g, "N4": X.x1, "N5": X.hb, "E6": X.v, "N6": X.x2, "N7": X.x3}
        STORE_LAG = {p: {"N5": 8, "N7": 9}.get(p, 7) for p in PASSES}
        WIDTH = {p: DH if p in ("N1", "E1", "N2", "E2") else DM for p in PASSES}
        IN_WIDTH = {p: DH if p in ("E1", "N2", "E2", "N3") else DM for p in PASSES}
        def before(p, passes):
            return ([q for q in NAMES[:NAMES.index(p)] if q in passes] or [None])[-1]

        block = ctx.enter_context(nc.Block())

        @block.sync
        def _(sp):
            for p, n in PASSES.items():
                load_weights(sp, p)
                edge = p[0] == "E"
                if p in ("E3", "E4"):
                    if p == "E4":
                        wait(sp, added.through("N4"))
                    sp.dma_start(gate[:, :, :].rearrange("p a n -> p (a n)"),
                                 par.gate[p == "E4"].rearrange("r d a -> (r d a)").partition_broadcast(128))\
                        .then_inc(consts_loaded, 16)
                if p == "E5":
                    wait(sp, y_ready.through("N5"))
                    sp.dma_start(bqkv.rearrange("p a n -> p (a n)"), par.b_qkv.partition_broadcast(128))\
                        .then_inc(consts_loaded, 16)
                if p in LOADS:
                    q = before(p, PASSES)
                    if q:
                        wait(sp, XIN_USED[q].through(q))
                    if p == "E6":
                        sp.wait_ge(softmax, 8)
                    if p != "N1":
                        maker = {"N2": "N1", "N3": "N2", "N4": "N3", "N5": "N4", "E6": "E5", "N6": "N5", "N7": "N6"}[p]
                        wait_all(sp, stored.through(maker))

                def load(step, p=p, edge=edge):
                    if step.c >= 4:
                        wait(sp, XIN_USED[p].free(p, step, 4))
                    at = (edge_rows if edge else node_rows)(LOADS[p], step)
                    s = loaded.slot(p, step)
                    sp.dma_start(xin[:, s, 0:IN_WIDTH[p]], at).then_inc(loaded.sem(p, step), 16)


                def load_residual(step, p=p):
                    s = res_in.slot(p, step)
                    if step.c >= 4:
                        wait(sp, y_ready.free(p, step, 4))
                    source = {"N3": x, "N5": X.x1, "N7": X.x3}[p]
                    sp.dma_start(res[:, s, :], node_rows(source, step)).then_inc(res_in.sem(p, step), 16)

                def store(step, p=p, edge=edge):
                    wait(sp, OUT_FILLED[p].done(p, step))
                    at = (edge_rows if edge else node_rows)(STORES[p], step)
                    sp.dma_start(at, outs[:, stored.slot(p, step), 0:WIDTH[p]]).then_inc(stored.sem(p, step), 16)

                if p in RESIDUAL:
                    q = before(p, RESIDUAL)
                    if q:
                        wait(sp, y_ready.through(q))
                    pipelined(sp, n, (0, load), (RESIDUAL[p], load_residual), (STORE_LAG[p], store))
                elif p in LOADS:
                    pipelined(sp, n, (0, load), (STORE_LAG[p], store))
                else:
                    pipelined(sp, n, (0, store))
            wait_all(sp, stored.through("N7"))

        @block.gpsimd
        def _(pool):
            pool.sem_inc(product.sem, 2)
            pool.sem_inc(evacuated.sem, 2)
            pool.sem_inc(finished.sem, 4)
            for s in range(4):
                pool.sem_inc(stored.sems[s], 16)

            nc.gpsimd.memset(half[:, :], -0.5).then_inc(half_set, 1)
            pool.wait_ge(half_set, 1)
            nc.gpsimd.memset(zero[:, :], 0.0).then_inc(zero_set, 1)

            def gather(p, step, ring, tile, width, table, source, column, copied):
                s = ring.slot(p, step)
                if p not in LISTED:
                    nc.gpsimd.tensor_copy(column[:, s:s + 1], col(table, step)).then_inc(copied.sem, 1)
                    wait(pool, copied.done(p, step))
                    settle(pool)
                pool.indirect_dma_start(
                    out=tile[:, s, 0:width], out_offset=None, in_=source,
                    in_offset=bass.IndirectOffsetOnAxis(ap=column[:, s:s + 1], axis=0),
                    bounds_check=source.shape[0] - 1, oob_is_err=False).then_inc(ring.sem(p, step), 16)

            for p, n in PASSES.items():
                src_pass = {"E1": "N1", "N2": "E1", "E2": "N2", "N3": "E2", "E3": "N3", "N4": "E3", "E4": "N4",
                            "N5": "E4", "E5": "N5", "N6": "E6", "E7": "N6", "N7": "E7"}.get(p)
                if not src_pass:
                    continue
                wait_all(pool, stored.through(src_pass))
                source = STORES[src_pass]
                edge = p[0] == "E"
                q = before(p, PASSES)
                if edge:
                    wait(pool, XIN_USED[q].through(q))
                qa = before(p, AGG_USED)
                if p in AGG_USED and qa:
                    wait(pool, AGG_USED[qa].through(qa))
                if p == "N5":
                    wait(pool, gated.through("E4"))

                def gathers(step, p=p, source=source, edge=edge):
                    if p in LISTED:
                        wait(pool, listed.done(p, step))
                        settle(pool)
                        if p == "N2":
                            gather(p, step, agg_in, agg, DH, P.last_D, source, list_col[0], None)
                        else:
                            gather(p, step, agg_in, agg, DM, P.last_S0, source, list_col[0], None)
                        return
                    if edge:
                        if step.c >= 4:
                            wait(pool, XIN_USED[p].free(p, step, 4))
                            settle(pool)
                        side = P.S if p in ("E3", "E4") else P.D
                        gather(p, step, gathered, xin, IN_WIDTH[p], side.gather, source, list_col[0], list_copied)
                        if p == "E5":
                            gather(p, step, agg_in, agg, DM, P.receivers, source, list_col[1], list_copied2)
                        return
                    width = DH if p == "N3" else DM
                    if p in ("N3", "N7"):
                        if step.c >= 4:
                            wait(pool, AGG_USED[p].free(p, step, 4))
                            settle(pool)
                        nc.gpsimd.memset(agg[:, agg_in.slot(p, step), 0:width], 0.0).then_inc(prefilled.sem, 1)
                    wait(pool, (prefilled if p in ("N3", "N7") else bias_filled).done(p, step))
                    settle(pool)
                    gather(p, step, agg_in, agg, width, P.last_S0 if p == "N5" else P.last_D, source, list_col[0],
                           list_copied)
                    if p == "N5":
                        wait(pool, added.free(p, step, 4) if step.c >= 4 else added.through("N4"))
                        settle(pool)
                        nc.gpsimd.memset(agg2[:, agg2_in.slot(p, step), :], 0.0).then_inc(prefilled2.sem, 1)
                        wait(pool, prefilled2.done(p, step))
                        settle(pool)
                        gather(p, step, agg2_in, agg2, DM, P.last_S1, source, list_col[1], list_copied2)

                def gather_second(step, p=p, source=source):
                    wait(pool, listed2.done(p, step))
                    settle(pool)
                    gather(p, step, agg2_in, agg2, DM, P.last_S1, source, list_col[1], None)

                def inverse_norm(step, p=p):
                    s = step.c % 4
                    wait(pool, squared.done(p, step))
                    settle(pool)
                    nc.gpsimd.tensor_scalar(sq[:, s:s + 1], sq[:, s:s + 1], 1e-24, None, ALU.max).then_inc(bounded.sem, 1)
                    wait(pool, bounded.done(p, step))
                    nc.gpsimd.tensor_tensor(rn[:, s:s + 1], sq[:, s:s + 1], half[:, 0:1], ALU.pow).then_inc(inv_norm.sem, 1)

                def inverse_std(step, p=p):
                    s = step.c % 4
                    wait(pool, var_ready.done(p, step))
                    nc.gpsimd.tensor_tensor(rstd[:, s:s + 1], ve[:, s:s + 1], half[:, 0:1], ALU.pow).then_inc(rstd_ready.sem, 1)

                stages = [(0, gathers)]
                if p == "N4":
                    stages += [(1, gather_second)]
                if p == "N3":
                    stages += [(4, inverse_norm)]
                if p in NORMED:
                    stages += [({"N3": 6, "N5": 5, "N6": 4, "N7": 6}[p], inverse_std)]
                pipelined(pool, n, *stages)

        @block.tensor
        def _(pe):

            def transpose(p, step, tile, width, bank=None, tell=True):
                s = step.c % 2 if bank is None else bank
                for k in range(width // 128):
                    last = nc.tensor.transpose(pT[:, s, k * 128:(k + 1) * 128], tile[:, k * 128:(k + 1) * 128], P.ident[:, :])
                if tell:
                    last.then_inc(transposed.sem, 1)

            def multiply(dst, hi, lo, w_hi, w_lo, k_tiles, width):
                for k in range(k_tiles):
                    at = slice(k * 128, (k + 1) * 128)
                    nc.tensor.matmul(dst[:, 0:width], hi[:, at], w_hi(k), start=k == 0, stop=False)
                    nc.tensor.matmul(dst[:, 0:width], hi[:, at], w_lo(k), start=False, stop=False)
                    last = nc.tensor.matmul(dst[:, 0:width], lo[:, at], w_hi(k), start=False, stop=k == k_tiles - 1)
                return last

            for p, n in PASSES.items():
                if p not in TRANSPOSED:
                    continue
                q = before(p, TRANSPOSED)
                if q:
                    wait(pe, PT_USED[q].through(q))
                    wait(pe, evacuated.through(q))
                if p in ("E3", "E4"):
                    type0 = pe.value_load(P.type0_tiles[0:1, 0:1], min_val=0, max_val=S_TILES)
                need_weights(pe, WEIGHTS_USED[p])

                def turn(step, p=p):
                    s4, s2 = step.c % 4, step.c % 2
                    if p in ("N1", "N4", "N5", "N7", "E7"):
                        wait(pe, xin_in(p).done(p, step))
                        tile = xin[:, xin_in(p).slot(p, step), :]
                    elif p == "N3":
                        wait(pe, summed.done(p, step))
                        tile = scan[:, s2, :]
                    else:
                        wait(pe, scaled.done(p, step))
                        tile = y[:, s4, :]
                    if step.c >= 2:
                        wait(pe, PT_USED[p].free(p, step, 2))
                    transpose(p, step, tile, DH if p in ("E1", "E2", "N3") else DM)

                def turn_back(step, p=p):
                    s2 = step.c % 2
                    wait(pe, scanned.done(p, step))
                    wait(pe, evacuated.free(p, step, 2))
                    for k in range(DH // 128):
                        last = nc.tensor.transpose(pM[:, s2, k * 128:(k + 1) * 128], scan[:, s2, k * 128:(k + 1) * 128],
                                                   P.ident[:, :])
                    last.then_inc(product.sem, 1)

                def dense(step, p=p):
                    s2 = step.c % 2
                    wait(pe, split.done(p, step))
                    wait(pe, evacuated.free(p, step, 2))
                    if p in ("E3", "E4"):
                        kind = step.t >= type0

                        def w(half_):
                            return lambda k: half_[:, bass.ds(kind, 1), k, :].rearrange("p a n -> p (a n)")
                        w_hi, w_lo = w(we_hi), w(we_lo)
                    elif p in ("E7", "N7"):
                        place = 0 if p == "E7" else 1
                        w_hi, w_lo = (lambda k: we_hi[:, place, k, :]), (lambda k: we_lo[:, place, k, :])
                    else:
                        width = DH if p == "N1" else DM
                        w_hi, w_lo = (lambda k: wn_hi[:, k, 0:width]), (lambda k: wn_lo[:, k, 0:width])
                    multiply(pM[:, s2, :], xT_hi[:, s2, :], xT_lo[:, s2, :], w_hi, w_lo,
                             2 if p == "N3" else 4, DH if p == "N1" else DM).then_inc(product.sem, 1)

                def turn_pair(step, p=p):
                    wait(pe, xin_in(p).done(p, step))
                    wait(pe, agg_in.done(p, step))
                    if step.c >= 1:
                        wait(pe, split.free(p, step, 1))
                    transpose(p, step, xin[:, xin_in(p).slot(p, step), :], DM, 0, False)
                    transpose(p, step, agg[:, agg_in.slot(p, step), :], DM, 1)

                def qkv(step, p=p):
                    s2 = step.c % 2
                    wait(pe, split.done(p, step))
                    if step.c >= 1:
                        wait(pe, v_added.free(p, step, 1))
                    multiply(pM[:, 4, :], xT_hi[:, s2, :], xT_lo[:, s2, :], lambda k: we_hi[:, 2, k, :],
                             lambda k: we_lo[:, 2, k, :], 4, DM).then_inc(v_done.sem, 1)
                    if step.c >= 2:
                        wait(pe, qk_added.free(p, step, 2))
                    multiply(pM[:, s2, :], xT_hi[:, s2, :], xT_lo[:, s2, :], lambda k: we_hi[:, 1, k, :],
                             lambda k: we_lo[:, 1, k, :], 4, DM)
                    multiply(pM[:, 2 + s2, :], rT_hi[:, s2, :], rT_lo[:, s2, :], lambda k: we_hi[:, 0, k, :],
                             lambda k: we_lo[:, 0, k, :], 4, DM).then_inc(product.sem, 1)

                def turn_scores(step, p=p):
                    wait(pe, scored.done(p, step))
                    if step.c >= 1:
                        wait(pe, score_kept.free(p, step, 1))
                    nc.tensor.transpose(pM[0:HEADS, 5, 0:128], scores[:, step.c % 2, :], P.ident[:, :])\
                        .then_inc(score_T.sem, 1)

                def turn_att(step, p=p):
                    s2 = step.c % 2
                    wait(pe, att_cut.done(p, step))
                    if step.c >= 2:
                        wait(pe, scaled.free(p, step, 2))
                    settle(pe)
                    nc.tensor.transpose(pM[:, 4 + s2, 0:HEADS], att[:, s2, :], P.ident[0:HEADS, 0:HEADS])\
                        .then_inc(att_T.sem, 1)

                if p in ("E1", "E2"):
                    pipelined(pe, n, (0, turn), (1, turn_back))
                elif p == "E5":
                    pipelined(pe, n, (0, turn_pair), (1, qkv), (2, turn_scores))
                elif p == "E6":
                    pipelined(pe, n, (0, turn_att), (1, turn), (3, dense))
                elif p in ("E3", "E4", "E7"):
                    pipelined(pe, n, (0, turn), (2, dense))
                else:
                    pipelined(pe, n, (0, turn), (1, dense))

        @block.scalar
        def _(act):
            for a, source in (
                    (b1, par.b1), (b2, par.b2), (bias1, par.bias1), (bias2, par.bias2), (bff, par.b_ff), (b3, par.b3)):
                act.dma_start(a[:, :], source.partition_broadcast(128)).then_inc(consts_loaded, 16)
            act.wait_ge(zero_set, 1)
            for p, n in PASSES.items():
                split_weights_high(act, p)
                if p == "N4":
                    act.wait_ge(consts_loaded, 7 * 16)
                if p in DENSE and p != "N1":
                    wait(act, product.through(before(p, TRANSPOSED)))

                def take_high(step, p=p):
                    s2 = step.c % 2
                    wait(act, scanned.done(p, step) if p in SCANNED else transposed.done(p, step))
                    wait(act, product.free(p, step, 2))
                    width = DH if p == "N3" else DM
                    source = scan[:, s2, 0:width] if p in SCANNED else pT[:, s2, 0:width]
                    nc.scalar.activation(xT_hi[:, s2, 0:width], source, ACT.Copy).then_inc(high.sem, 1)

                def take_high_pair(step, p=p):
                    s2 = step.c % 2
                    wait(act, transposed.done(p, step))
                    wait(act, product.free(p, step, 2))
                    nc.scalar.activation(xT_hi[:, s2, :], pT[:, 0, :], ACT.Copy)
                    nc.scalar.activation(rT_hi[:, s2, :], pT[:, 1, :], ACT.Copy).then_inc(high.sem, 1)

                def h_out(step, p=p):
                    wait(act, product.done(p, step))
                    wait(act, stored.free(p, step))
                    settle(act)
                    nc.scalar.activation(outs[:, stored.slot(p, step), 0:DH], pM[:, step.c % 2, 0:DH], ACT.Copy,
                                         scale=col(P.dinv, step)).then_inc(evacuated.sem, 1)

                def scale_edge(step, p=p):
                    s = step.c % 4
                    wait(act, xin_in(p).done(p, step))
                    if step.c >= 4:
                        wait(act, transposed.free(p, step, 4))
                    width = IN_WIDTH[p]
                    if p in ("E3", "E4"):
                        wait(act, gated.done(p, step))
                        nc.scalar.activation(g[:, s:s + 1], z[:, s:s + 1], ACT.Sigmoid).then_inc(sigmoid.sem, 1)
                        wait(act, sigmoid.done(p, step))
                        scale = g[:, s:s + 1]
                    else:
                        settle(act)
                        scale = col(P.weights, step)
                    nc.scalar.activation(y[:, s, 0:width], xin[:, xin_in(p).slot(p, step), 0:width], ACT.Copy, scale=scale)\
                        .then_inc(scaled.sem, 1)

                def copy_out(step, p=p):
                    wait(act, product.done(p, step))
                    wait(act, stored.free(p, step))
                    nc.scalar.activation(outs[:, stored.slot(p, step), 0:WIDTH[p]], pM[:, step.c % 2, 0:WIDTH[p]], ACT.Copy)\
                        .then_inc(evacuated.sem, 1)

                def prefill(step, p=p):
                    if step.c >= 4:
                        wait(act, AGG_USED[p].free(p, step, 4))
                    bias = bias2 if p == "N5" else bff
                    nc.scalar.activation(agg[:, agg_in.slot(p, step), :], bias[:, :], ACT.Copy).then_inc(bias_filled.sem, 1)

                def list_nodes(step, p=p):
                    s = agg_in.slot(p, step)
                    if step.c >= 4:
                        wait(act, agg_in.done(p, step.back(4)))
                        wait(act, AGG_USED[p].free(p, step, 4))
                    if p == "N2":
                        nc.scalar.activation(agg[:, s, 0:DH], zero[:, 0:1].broadcast_to([128, DH]), ACT.Copy)
                    else:
                        nc.scalar.activation(agg[:, s, :], bias1[:, :], ACT.Copy)
                    nc.scalar.activation(list_col[0][:, s:s + 1], col(P.last_D if p == "N2" else P.last_S0, step), ACT.Copy)\
                        .then_inc(listed.sem, 1)

                def list_second(step, p=p):
                    s = agg2_in.slot(p, step)
                    if step.c >= 4:
                        wait(act, agg2_in.done(p, step.back(4)))
                        wait(act, added.free(p, step, 4))
                    nc.scalar.activation(agg2[:, s, :], zero[:, 0:1].broadcast_to([128, DM]), ACT.Copy)
                    nc.scalar.activation(list_col[1][:, s:s + 1], col(P.last_S1, step), ACT.Copy).then_inc(listed2.sem, 1)

                def relu_out(step, p=p):
                    wait(act, added.done(p, step))
                    wait(act, stored.free(p, step))
                    nc.scalar.activation(outs[:, stored.slot(p, step), :], y[:, step.c % 4, :], ACT.Relu)\
                        .then_inc(finished.sem, 1)

                def sum_squares(step, p=p):
                    s = step.c % 4
                    wait(act, evacuated.done(p, step))
                    if step.c >= 1:
                        wait(act, squared.free(p, step, 1))
                    nc.scalar.activation(prod[:, :], y[:, s, :], ACT.Square, accum_out=sq[:, s:s + 1])\
                        .then_inc(squared.sem, 1)

                def silu(step, p=p):
                    wait(act, biased.done(p, step))
                    if step.c >= 2:
                        wait(act, y_ready.free(p, step, 2))
                    nc.scalar.activation(scan[:, step.c % 2, :], agg[:, agg_in.slot(p, step), :], ACT.Silu).then_inc(silued.sem, 1)

                def norm_out(step, p=p):
                    s = step.c % 4
                    wait(act, shift_ready.done(p, step))
                    wait(act, stored.free(p, step))
                    nc.scalar.activation(outs[:, stored.slot(p, step), :], y[:, s, :], ACT.Identity,
                                         scale=rstd[:, s:s + 1], bias=nb[:, s:s + 1]).then_inc(finished.sem, 1)

                def keep_scores(step, p=p):
                    wait(act, score_T.done(p, step))
                    settle(act)
                    nc.scalar.activation(srow[:, bass.ds(step.number(0, 128), 128)], pM[0:HEADS, 5, 0:128], ACT.Copy,
                                         scale=float(DK) ** -0.5).then_inc(score_kept.sem, 1)

                def cut_att(step, p=p):
                    if step.c >= 2:
                        wait(act, att_T.free(p, step, 2))
                        settle(act)
                    nc.scalar.activation(att[:, step.c % 2, :], srow[:, bass.ds(step.number(0, 128), 128)], ACT.Copy)\
                        .then_inc(att_cut.sem, 1)

                if p in ("N2", "N4", "N5", "N6") and before(p, AGG_USED):
                    qa = before(p, AGG_USED)
                    wait(act, AGG_USED[qa].through(qa))
                    wait_all(act, agg_in.through(qa))
                if p in LISTED:
                    wait_all(act, gathered.through(p))
                if p == "N1":
                    pipelined(act, n, (0, take_high), (2, h_out))
                elif p in ("E1", "E2"):
                    pipelined(act, n, (0, scale_edge), (2, copy_out))
                elif p == "N2":
                    pipelined(act, n, (0, list_nodes))
                elif p == "N3":
                    pipelined(act, n, (6, norm_out), (0, take_high), (2, sum_squares))
                elif p in ("E3", "E4"):
                    pipelined(act, n, (0, scale_edge), (1, take_high))
                elif p == "N4":
                    pipelined(act, n, (0, list_nodes), (1, list_second), (2, take_high), (5, relu_out))
                elif p == "N5":
                    pipelined(act, n, (0, prefill), (2, take_high), (7, norm_out))
                elif p == "E5":
                    pipelined(act, n, (0, take_high_pair), (2, keep_scores))
                    act.wait_ge(softmax, 4)
                    nc.scalar.activation(srow[:, :], srow[:, :], ACT.Exp).then_inc(exps, 1)
                    act.wait_ge(softmax, 8)
                elif p == "E6":
                    pipelined(act, n, (0, cut_att), (2, take_high))
                elif p == "N6":
                    pipelined(act, n, (6, norm_out), (0, prefill))
                elif p == "E7":
                    pipelined(act, n, (3, copy_out), (0, take_high))
                elif p == "N7":
                    pipelined(act, n, (0, take_high), (3, silu), (7, norm_out))

        @block.vector
        def _(dve):
            for p, n in PASSES.items():
                split_weights_low(dve, p)
                if p == "N2":
                    dve.wait_ge(consts_loaded, 6 * 16)
                dp = DM if p not in ("E1", "E2") else DH
                if p in ("E3", "E4"):
                    type0 = dve.value_load(P.type0_tiles[0:1, 0:1], min_val=0, max_val=S_TILES)
                    dve.wait_ge(consts_loaded, (7 if p == "E3" else 8) * 16)

                if p == "E5":
                    dve.wait_ge(consts_loaded, 9 * 16)

                def take_low(step, p=p):
                    s2 = step.c % 2
                    wait(dve, high.done(p, step))
                    width = DH if p == "N3" else DM
                    source = scan[:, s2, 0:width] if p in SCANNED else pT[:, s2, 0:width]
                    nc.vector.tensor_tensor(xT_lo[:, s2, 0:width], source, xT_hi[:, s2, 0:width].bitcast(F32),
                                            ALU.subtract).then_inc(split.sem, 1)

                def take_low_pair(step, p=p):
                    s2 = step.c % 2
                    wait(dve, high.done(p, step))
                    nc.vector.tensor_tensor(xT_lo[:, s2, :], pT[:, 0, :], xT_hi[:, s2, :].bitcast(F32), ALU.subtract)
                    nc.vector.tensor_tensor(rT_lo[:, s2, :], pT[:, 1, :], rT_hi[:, s2, :].bitcast(F32), ALU.subtract)\
                        .then_inc(split.sem, 1)

                def run_sums(step, p=p, dp=dp):
                    s2 = step.c % 2
                    side = P.S if p in ("E3", "E4") else P.D
                    wait(dve, transposed.done(p, step))
                    if step.c >= 1:
                        wait(dve, scanned.free(p, step, 1))
                    if step.c >= 2:
                        wait(dve, product.free(p, step, 2) if p in ("E1", "E2") else split.free(p, step, 2))
                    for k in range(dp // 128):
                        last = nc.vector.tensor_tensor_scan(
                            scan[:, s2, k * 128:(k + 1) * 128], side.same_run[:, bass.ds(step.number(0, 128), 128)],
                            pT[:, s2, k * 128:(k + 1) * 128],
                            0.0 if step.c == 0 and step.i is None else scan[:, 1 - s2, k * 128 + 127:k * 128 + 128],
                            ALU.mult, ALU.add)
                    last.then_inc(scanned.sem, 1)

                def sum_rows(step, p=p):
                    s = step.c % 4
                    wait(dve, xin_in(p).done(p, step))
                    wait(dve, agg_in.done(p, step))
                    width = DM if p == "N6" else DH
                    if p == "N3":
                        if step.c >= 2:
                            wait(dve, transposed.free(p, step, 2))
                        into = scan[:, step.c % 2, 0:width]
                    else:
                        wait(dve, finished.free(p, step, 4))
                        into = y[:, s, 0:width]
                    nc.vector.tensor_tensor(into, xin[:, xin_in(p).slot(p, step), 0:width],
                                            agg[:, agg_in.slot(p, step), 0:width], ALU.add).then_inc(summed.sem, 1)

                def scale_rows(step, p=p):
                    s = step.c % 4
                    wait(dve, summed.done(p, step))
                    nc.vector.scalar_tensor_tensor(y[:, s, 0:DH], y[:, s, 0:DH], col(P.dinv, step), b1[:, :],
                                                   ALU.mult, ALU.add).then_inc(added.sem, 1)

                def relu_scaled(step, p=p):
                    wait(dve, added.done(p, step))
                    wait(dve, stored.free(p, step))
                    nc.vector.tensor_scalar(outs[:, stored.slot(p, step), 0:DH], y[:, step.c % 4, 0:DH], 0.0,
                                            col(P.dinv, step), ALU.max, ALU.mult).then_inc(finished.sem, 1)

                def gcn_out(step, p=p):
                    wait(dve, product.done(p, step))
                    wait(dve, finished.free(p, step, 4))
                    nc.vector.scalar_tensor_tensor(y[:, step.c % 4, :], pM[:, step.c % 2, :], col(P.dinv, step), b2[:, :],
                                                   ALU.mult, ALU.add).then_inc(evacuated.sem, 1)

                def normalise(step, p=p):
                    s = step.c % 4
                    wait(dve, inv_norm.done(p, step))
                    wait(dve, res_in.done(p, step))
                    nc.vector.scalar_tensor_tensor(y[:, s, :], y[:, s, :], rn[:, s:s + 1], res[:, res_in.slot(p, step), :],
                                                   ALU.mult, ALU.add).then_inc(y_ready.sem, 1)

                def statistics(step, p=p):
                    s = step.c % 4
                    wait(dve, (summed if p == "N6" else y_ready).done(p, step))
                    nc.vector.bn_stats(stats[:, s, :], y[:, s, :]).then_inc(bn_done.sem, 1)

                def variance(step, p=p):
                    s = step.c % 4
                    wait(dve, bn_done.done(p, step))
                    settle(dve)
                    nc.vector.bn_aggr(mv[:, s, :], stats[:, s, :]).then_inc(mean_ready.sem, 1)

                def add_epsilon(step, p=p):
                    s = step.c % 4
                    wait(dve, mean_ready.done(p, step))
                    nc.vector.tensor_scalar(ve[:, s:s + 1], mv[:, s, 1:2], 1e-5, None, ALU.add).then_inc(var_ready.sem, 1)

                def shift(step, p=p):
                    s = step.c % 4
                    wait(dve, rstd_ready.done(p, step))
                    nc.vector.scalar_tensor_tensor(nb[:, s:s + 1], mv[:, s, 0:1], -1.0, rstd[:, s:s + 1],
                                                   ALU.mult, ALU.mult).then_inc(shift_ready.sem, 1)

                def dot_gate(step, p=p):
                    s = step.c % 4
                    wait(dve, xin_in(p).done(p, step))
                    if step.c >= 1:
                        wait(dve, gated.free(p, step, 1))
                    if step.c >= 4:
                        wait(dve, sigmoid.free(p, step, 4))
                    kind = step.t >= type0
                    nc.vector.scalar_tensor_tensor(
                        prod[:, :], xin[:, xin_in(p).slot(p, step), :], 1.0,
                        gate[:, bass.ds(kind, 1), :].rearrange("p a n -> p (a n)"),
                        ALU.mult, ALU.mult, accum_out=z[:, s:s + 1]).then_inc(gated.sem, 1)

                def message_out(step, p=p):
                    wait(dve, product.done(p, step))
                    wait(dve, stored.free(p, step))
                    bias = {"E3": bias1, "E4": bias2, "E6": bff}[p]
                    scale = 1.0 if p == "E6" else col(P.is_type0, step)
                    nc.vector.scalar_tensor_tensor(outs[:, stored.slot(p, step), :], bias[:, :], scale, pM[:, step.c % 2, :],
                                                   ALU.mult, ALU.add).then_inc(evacuated.sem, 1)

                def add_first(step, p=p):
                    wait(dve, product.done(p, step))
                    wait(dve, agg_in.done(p, step))
                    wait(dve, finished.free(p, step, 4))
                    nc.vector.tensor_tensor(y[:, step.c % 4, :], pM[:, step.c % 2, :], agg[:, agg_in.slot(p, step), :],
                                            ALU.add).then_inc(evacuated.sem, 1)

                def add_second(step, p=p):
                    s = step.c % 4
                    wait(dve, evacuated.done(p, step))
                    wait(dve, agg2_in.done(p, step))
                    nc.vector.tensor_tensor(y[:, s, :], y[:, s, :], agg2[:, agg2_in.slot(p, step), :], ALU.add)\
                        .then_inc(added.sem, 1)

                def add_residual(step, p=p):
                    s = step.c % 4
                    wait(dve, added.done(p, step))
                    wait(dve, res_in.done(p, step))
                    nc.vector.tensor_tensor(y[:, s, :], y[:, s, :], res[:, res_in.slot(p, step), :], ALU.add)\
                        .then_inc(y_ready.sem, 1)

                def add_values(step, p=p):
                    wait(dve, v_done.done(p, step))
                    wait(dve, stored.free(p, step))
                    nc.vector.tensor_tensor(outs[:, stored.slot(p, step), :], pM[:, 4, :], bqkv[:, 2, :], ALU.add)\
                        .then_inc(v_added.sem, 1)

                def add_qk(step, p=p):
                    s = step.c % 4
                    s2 = step.c % 2
                    wait(dve, product.done(p, step))
                    if step.c >= 1:
                        wait(dve, scored.free(p, step, 1))
                    nc.vector.tensor_tensor(y[:, s, :], pM[:, s2, :], bqkv[:, 1, :], ALU.add)
                    nc.vector.tensor_tensor(prod[:, :], pM[:, 2 + s2, :], bqkv[:, 0, :], ALU.add).then_inc(qk_added.sem, 1)

                def multiply_qk(step, p=p):
                    s = step.c % 4
                    wait(dve, qk_added.done(p, step))
                    nc.vector.tensor_tensor(y[:, s, :], y[:, s, :], prod[:, :], ALU.mult).then_inc(multiplied.sem, 1)

                def score(step, p=p):
                    wait(dve, multiplied.done(p, step))
                    if step.c >= 2:
                        wait(dve, score_T.free(p, step, 2))
                    nc.vector.reduce_sum(scores[:, step.c % 2, :], y[:, step.c % 4, :].rearrange("p (h d) -> p h d", h=HEADS),
                                         AX.X).then_inc(scored.sem, 1)

                def weigh_values(step, p=p):
                    s = step.c % 4
                    wait(dve, xin_in(p).done(p, step))
                    wait(dve, att_T.done(p, step))
                    if step.c >= 4:
                        wait(dve, transposed.free(p, step, 4))
                    nc.vector.tensor_tensor(
                        y[:, s, :].rearrange("p (h d) -> p h d", h=HEADS),
                        xin[:, xin_in(p).slot(p, step), :].rearrange("p (h d) -> p h d", h=HEADS),
                        pM[:, 4 + step.c % 2, 0:HEADS].unsqueeze(2).broadcast_to([128, HEADS, DK]), ALU.mult)\
                        .then_inc(scaled.sem, 1)

                def sage_sum(step, p=p):
                    wait(dve, product.done(p, step))
                    wait(dve, agg_in.done(p, step))
                    tile = agg[:, agg_in.slot(p, step), :]
                    nc.vector.scalar_tensor_tensor(tile, tile, col(P.rdeg, step), pM[:, step.c % 2, :],
                                                   ALU.mult, ALU.add).then_inc(evacuated.sem, 1)

                def sage_bias(step, p=p):
                    tile = agg[:, agg_in.slot(p, step), :]
                    wait(dve, evacuated.done(p, step))
                    nc.vector.tensor_tensor(tile, tile, b3[:, :], ALU.add).then_inc(biased.sem, 1)

                def sage_residual(step, p=p):
                    s = step.c % 4
                    wait(dve, silued.done(p, step))
                    wait(dve, res_in.done(p, step))
                    wait(dve, finished.free(p, step, 4))
                    nc.vector.tensor_tensor(y[:, s, :], scan[:, step.c % 2, :], res[:, res_in.slot(p, step), :], ALU.add)\
                        .then_inc(y_ready.sem, 1)

                def soft_max(dve):
                    E = D_TILES * 128
                    flat = rows[0:HEADS, :, :, :].rearrange("p a b n -> p (a b n)")
                    run = flat[:, 0:E]
                    cut = flat[:, E:E + E // 2 + 2].bitcast(BF16)[:, 0:E + 1]
                    same = P.D.same_run[0:HEADS, :]
                    wait(dve, score_kept.through("E5"))
                    nc.vector.tensor_scalar(cut, same[:, :], -1.0, 1e30, ALU.add, ALU.mult).then_inc(softmax, 1)
                    dve.wait_ge(softmax, 1)
                    nc.vector.tensor_tensor_scan(run, cut[:, 0:E], srow[:, :], -1e30, ALU.add, ALU.max).then_inc(softmax, 1)
                    dve.wait_ge(softmax, 2)
                    nc.vector.tensor_tensor_scan(run[:, ::-1], cut[:, E:0:-1], run[:, ::-1], -1e30, ALU.add, ALU.max)\
                        .then_inc(softmax, 1)
                    dve.wait_ge(softmax, 3)
                    nc.vector.tensor_tensor(srow[:, :], srow[:, :], run, ALU.subtract).then_inc(softmax, 1)
                    dve.wait_ge(exps, 1)
                    nc.vector.tensor_tensor_scan(run, same[:, 0:E], srow[:, :], 0.0, ALU.mult, ALU.add).then_inc(softmax, 1)
                    dve.wait_ge(softmax, 5)
                    nc.vector.tensor_tensor_scan(run[:, ::-1], same[:, E:0:-1], run[:, ::-1], 0.0, ALU.mult, ALU.max)\
                        .then_inc(softmax, 1)
                    dve.wait_ge(softmax, 6)
                    nc.vector.reciprocal(run, run).then_inc(softmax, 1)
                    dve.wait_ge(softmax, 7)
                    nc.vector.tensor_tensor(srow[:, :], srow[:, :], run, ALU.mult).then_inc(softmax, 1)

                if p == "N1":
                    pipelined(dve, n, (0, take_low))
                elif p in ("E1", "E2"):
                    pipelined(dve, n, (0, run_sums))
                elif p == "N2":
                    pipelined(dve, n, (0, sum_rows), (1, scale_rows), (2, relu_scaled))
                elif p == "N3":
                    pipelined(dve, n, (4, statistics), (0, sum_rows), (4, variance), (1, take_low), (4, add_epsilon),
                              (2, gcn_out), (3, normalise), (5, shift))
                elif p in ("E3", "E4"):
                    pipelined(dve, n, (0, dot_gate), (2, take_low), (1, run_sums), (3, message_out))
                elif p == "N4":
                    pipelined(dve, n, (0, take_low), (1, add_first), (2, add_second))
                elif p == "N5":
                    pipelined(dve, n, (3, statistics), (0, take_low), (3, variance), (2, add_second),
                              (3, add_epsilon), (4, shift), (1, add_first), (2, add_residual))
                elif p == "E5":
                    pipelined(dve, n, (0, take_low_pair), (1, add_values), (1, add_qk), (1, multiply_qk), (1, score))
                    soft_max(dve)
                elif p == "E6":
                    pipelined(dve, n, (0, weigh_values), (1, run_sums), (2, take_low), (3, message_out))
                elif p == "N6":
                    pipelined(dve, n, (1, statistics), (3, shift), (1, variance), (0, sum_rows), (1, add_epsilon))
                elif p == "E7":
                    pipelined(dve, n, (0, run_sums), (1, take_low))
                elif p == "N7":
                    pipelined(dve, n, (5, statistics), (0, take_low), (5, variance), (1, sage_sum),
                              (5, add_epsilon), (4, sage_residual), (6, shift), (2, sage_bias))


def gnn_kernel(nc, x, src, dst, edge_type, edge_weight, par, out):
    ctx = ExitStack()
    with ctx:
        def sb(name, shape, dt=F32):
            return ctx.enter_context(nc.sbuf_tensor(name, shape, dt))

        def dram(name, rows, width):
            return nc.dram_tensor("rows_" + name, [rows, width], F32).ap()

        P = Named()
        P.ident = sb("ident", [128, 128])
        P.D = Ordering(D_TILES, NODE_COLS, sb("gather_D", [128, D_TILES], I32),
                       sb("same_run_D", [128, D_TILES * 128 + 1], BF16))
        P.S = Ordering(S_TILES, 2 * NODE_COLS, sb("gather_S", [128, S_TILES], I32),
                       sb("same_run_S", [128, S_TILES * 128 + 1], BF16))
        P.receivers, P.weights = sb("receivers", [128, D_TILES], I32), sb("weights", [128, D_TILES])
        P.type0_tiles, P.is_type0 = sb("type0_tiles", [128, 1], I32), sb("is_type0", [128, S_TILES])
        P.last_D, P.last_S0, P.last_S1 = (sb(n, [128, NODE_STEPS], I32) for n in ("last_D", "last_S0", "last_S1"))
        P.dinv, P.rdeg = sb("dinv", [128, NODE_STEPS]), sb("rdeg", [128, NODE_STEPS])

        X = Named()
        X.h, X.g = dram("h", N, DH), dram("g", N, DH)
        X.x1, X.hb, X.x2, X.x3 = (dram(name, N, DM) for name in ("x1", "hb", "x2", "x3"))
        X.r1, X.r2 = (dram(name, D_TILES * 128, DH) for name in ("r1", "r2"))
        X.r3, X.r4 = (dram(name, S_TILES * 128, DM) for name in ("r3", "r4"))
        X.v, X.r5, X.r6 = (dram(name, D_TILES * 128, DM) for name in ("v", "r5", "r6"))
        X.mixed = [dram(f"mixed{l}", 8, 128 * DM) for l in range(2)]
        prepare(nc, P, src, dst, edge_type, edge_weight, X.mixed, par.att, par.basis)
        layers_block(nc, P, x, out, par, X)


_INS = ['x', 'src', 'dst', 'edge_type_2', 'edge_weight', 'L0_gnn_W1', 'L0_gnn_b1', 'L0_gnn_W2', 'L0_gnn_b2',
        'L1_gnn_basis1', 'L1_gnn_att1', 'L1_gnn_gate_w1', 'L1_gnn_root1', 'L1_gnn_bias1',
        'L1_gnn_basis2', 'L1_gnn_att2', 'L1_gnn_gate_w2', 'L1_gnn_root2', 'L1_gnn_bias2',
        'L2_gnn_W_qkv', 'L2_gnn_b_qkv', 'L2_gnn_W_ff', 'L2_gnn_b_ff', 'L3_gnn_W_l', 'L3_gnn_W_r', 'L3_gnn_b']
_TRANSPOSED = ('L2_gnn_W_qkv', 'L2_gnn_W_ff')


def kernel(**inputs):
    import numpy as _np
    import concourse.bacc as _bacc
    from concourse import mybir as _mybir
    from concourse.bass_utils import run_bass_kernel_spmd as _run

    nc = _bacc.Bacc("TRN2", target_bir_lowering=False, num_devices=1)
    arrays, aps = {}, {}
    for name in _INS:
        a = _np.asarray(inputs[name])
        a = _np.ascontiguousarray(a.T if name in _TRANSPOSED else a)
        arrays[f"in_{name}_dram"] = a
        aps[name] = nc.dram_tensor(f"in_{name}_dram", a.shape, _mybir.dt.from_np(a.dtype), kind="ExternalInput").ap()
    out = nc.dram_tensor("out_0_dram", (N, DM), F32, kind="ExternalOutput").ap()
    par = Named()
    par.W1, par.b1, par.W2, par.b2 = (aps[f"L0_gnn_{n}"] for n in ("W1", "b1", "W2", "b2"))
    par.basis, par.att, par.gate = ([aps[f"L1_gnn_{n}{l}"] for l in (1, 2)] for n in ("basis", "att", "gate_w"))
    par.root1, par.root2, par.bias1, par.bias2 = (aps[f"L1_gnn_{n}"] for n in ("root1", "root2", "bias1", "bias2"))
    par.W_qkv, par.b_qkv, par.W_ff, par.b_ff = (aps[f"L2_gnn_{n}"] for n in ("W_qkv", "b_qkv", "W_ff", "b_ff"))
    par.W_l, par.W_r, par.b3 = (aps[f"L3_gnn_{n}"] for n in ("W_l", "W_r", "b"))
    gnn_kernel(nc, aps["x"], aps["src"], aps["dst"], aps["edge_type_2"], aps["edge_weight"], par, out)
    r = _run(nc, [arrays], core_ids=[0])
    return r.results[0]["out_0_dram"]
```
